# Optimizing a Trainium2 kernel written in Bass

```python
import numpy as np
import jax
import jax.numpy as jnp

def _softmax(x, axis=-1):
    return jax.nn.softmax(x, axis=axis)

def _gelu(x):
    return jax.nn.gelu(x, approximate=True)

def _silu(x):
    return jax.nn.silu(x)

def _sigmoid(x):
    return jax.nn.sigmoid(x)

def _layernorm(x, axis=-1, eps=1e-05):
    m = jnp.mean(x, axis=axis, keepdims=True)
    v = jnp.var(x, axis=axis, keepdims=True)
    return (x - m) / jnp.sqrt(v + eps)

def _scatter_add(tgt, idx, src, axis=0):
    return tgt.at[idx].add(src)

def _segment_sum(src, seg, n):
    return jax.ops.segment_sum(src, seg, n)
kernel_name = 'mk_prb_d2_jaxref_r8_50283f'

def setup_inputs(seed: int=0):
    np.random.seed(seed)
    _w = jnp.asarray

    def _L0_attn_setup():
        import jax, jax.numpy as jnp
        import numpy as np
        B, L, E, D, H = (2, 256, 128, 128, 8)

        def _ln(x, g, b, eps=1e-05):
            m = jnp.mean(x, axis=-1, keepdims=True)
            v = jnp.mean((x - m) ** 2, axis=-1, keepdims=True)
            return (x - m) * jax.lax.rsqrt(v + eps) * g + b
        key = jax.random.key(seed)
        ks = jax.random.split(key, 10)
        s = 0.02

        def n(k, shape):
            return jax.random.normal(k, shape, jnp.float32) * s
        return {'emb': jax.random.normal(ks[0], (B, L, E), jnp.float32), 'Wa_w': n(ks[1], (H, D, E)), 'Wa_b': jnp.zeros((H, D), jnp.float32), 'Wb_w': n(ks[2], (H, D, E)), 'Wb_b': jnp.zeros((H, D), jnp.float32), 'C_w': n(ks[3], (H, D, D)), 'C_b': jnp.zeros((H, D), jnp.float32), 'D_w': n(ks[4], (D, E)), 'D_b': jnp.zeros((D,), jnp.float32), 'Wout_w': n(ks[5], (E, D)), 'Wout_b': jnp.zeros((E,), jnp.float32), 'hn_g': jnp.ones((H, D), jnp.float32), 'hn_b': jnp.zeros((H, D), jnp.float32), 'head_w': jnp.ones((H,), jnp.float32), 'ffn1_w': n(ks[6], (4 * E, E)), 'ffn1_b': jnp.zeros((4 * E,), jnp.float32), 'ffn2_w': n(ks[7], (E, 4 * E)), 'ffn2_b': jnp.zeros((E,), jnp.float32), 'proj_w': n(ks[8], (E, E)), 'proj_b': jnp.zeros((E,), jnp.float32), 'norm_g': jnp.ones((E,), jnp.float32), 'norm_b': jnp.zeros((E,), jnp.float32)}
    _L0_attn_in = _L0_attn_setup()

    def _L0_ffn_setup():
        import jax, jax.numpy as jnp
        import numpy as np
        HIDDEN = 128
        INTER = 512
        key = jax.random.key(seed)
        k1, k2, k3, k4, k5 = jax.random.split(key, 5)
        hidden_states = jax.random.normal(k1, (4, 256, HIDDEN), dtype=jnp.float32)
        W1 = jax.random.normal(k2, (HIDDEN, INTER), dtype=jnp.float32) * (1.0 / np.sqrt(HIDDEN))
        b1 = jax.random.normal(k3, (INTER,), dtype=jnp.float32) * 0.02
        W2 = jax.random.normal(k4, (INTER, HIDDEN), dtype=jnp.float32) * (1.0 / np.sqrt(INTER))
        b2 = jax.random.normal(k5, (HIDDEN,), dtype=jnp.float32) * 0.02
        return {'hidden_states': hidden_states, 'W1': W1, 'b1': b1, 'W2': W2, 'b2': b2}
    _L0_ffn_in = _L0_ffn_setup()

    def _L1_attn_setup():
        import jax, jax.numpy as jnp
        import numpy as np
        NUM_HEADS = 16
        key = jax.random.key(seed)
        ks = jax.random.split(key, 5)
        B, N, C = (4, 256, 128)
        s = 0.02
        return {'x': jax.random.normal(ks[0], (B, N, C), jnp.float32), 'w_qkv': jax.random.normal(ks[1], (C, 3 * C), jnp.float32) * s, 'b_qkv': jnp.zeros((3 * C,), jnp.float32), 'w_proj': jax.random.normal(ks[2], (C, C), jnp.float32) * s, 'b_proj': jnp.zeros((C,), jnp.float32)}
    _L1_attn_in = _L1_attn_setup()

    def _L1_ffn_setup():
        import jax, jax.numpy as jnp
        import numpy as np
        DIM = 128
        HIDDEN = 384
        SCALE = 1.0 / 127.0

        def _dequant(w_int, dtype):
            return w_int.astype(dtype) * jnp.asarray(SCALE, dtype)
        key = jax.random.key(seed)
        k_x, k_g, k_u, k_d = jax.random.split(key, 4)
        x = jax.random.normal(k_x, (4, 256, DIM), dtype=jnp.float32)
        w_gate = jax.random.randint(k_g, (HIDDEN, DIM), -127, 128, dtype=jnp.int32)
        w_up = jax.random.randint(k_u, (HIDDEN, DIM), -127, 128, dtype=jnp.int32)
        w_down = jax.random.randint(k_d, (DIM, HIDDEN), -127, 128, dtype=jnp.int32)
        return {'x': x, 'w_gate': w_gate, 'w_up': w_up, 'w_down': w_down}
    _L1_ffn_in = _L1_ffn_setup()
    _d = {'L0_attn_emb': _L0_attn_in['emb'], 'L0_attn_Wa_w': _L0_attn_in['Wa_w'], 'L0_attn_Wa_b': _L0_attn_in['Wa_b'], 'L0_attn_Wb_w': _L0_attn_in['Wb_w'], 'L0_attn_Wb_b': _L0_attn_in['Wb_b'], 'L0_attn_C_w': _L0_attn_in['C_w'], 'L0_attn_C_b': _L0_attn_in['C_b'], 'L0_attn_D_w': _L0_attn_in['D_w'], 'L0_attn_D_b': _L0_attn_in['D_b'], 'L0_attn_Wout_w': _L0_attn_in['Wout_w'], 'L0_attn_Wout_b': _L0_attn_in['Wout_b'], 'L0_attn_hn_g': _L0_attn_in['hn_g'], 'L0_attn_hn_b': _L0_attn_in['hn_b'], 'L0_attn_head_w': _L0_attn_in['head_w'], 'L0_attn_ffn1_w': _L0_attn_in['ffn1_w'], 'L0_attn_ffn1_b': _L0_attn_in['ffn1_b'], 'L0_attn_ffn2_w': _L0_attn_in['ffn2_w'], 'L0_attn_ffn2_b': _L0_attn_in['ffn2_b'], 'L0_attn_proj_w': _L0_attn_in['proj_w'], 'L0_attn_proj_b': _L0_attn_in['proj_b'], 'L0_attn_norm_g': _L0_attn_in['norm_g'], 'L0_attn_norm_b': _L0_attn_in['norm_b'], 'L0_ffn_W1': _L0_ffn_in['W1'], 'L0_ffn_b1': _L0_ffn_in['b1'], 'L0_ffn_W2': _L0_ffn_in['W2'], 'L0_ffn_b2': _L0_ffn_in['b2'], 'L1_attn_w_qkv': _L1_attn_in['w_qkv'], 'L1_attn_b_qkv': _L1_attn_in['b_qkv'], 'L1_attn_w_proj': _L1_attn_in['w_proj'], 'L1_attn_b_proj': _L1_attn_in['b_proj'], 'L1_ffn_w_gate': _L1_ffn_in['w_gate'], 'L1_ffn_w_up': _L1_ffn_in['w_up'], 'L1_ffn_w_down': _L1_ffn_in['w_down']}
    _x0 = _d['L0_attn_emb']
    _d['L0_attn_emb'] = jax.random.normal(jax.random.fold_in(jax.random.key(seed), 1), (8, 512, 128), dtype=_x0.dtype)
    del _x0
    return _d

def reference(L0_attn_emb, L0_attn_Wa_w, L0_attn_Wa_b, L0_attn_Wb_w, L0_attn_Wb_b, L0_attn_C_w, L0_attn_C_b, L0_attn_D_w, L0_attn_D_b, L0_attn_Wout_w, L0_attn_Wout_b, L0_attn_hn_g, L0_attn_hn_b, L0_attn_head_w, L0_attn_ffn1_w, L0_attn_ffn1_b, L0_attn_ffn2_w, L0_attn_ffn2_b, L0_attn_proj_w, L0_attn_proj_b, L0_attn_norm_g, L0_attn_norm_b, L0_ffn_W1, L0_ffn_b1, L0_ffn_W2, L0_ffn_b2, L1_attn_w_qkv, L1_attn_b_qkv, L1_attn_w_proj, L1_attn_b_proj, L1_ffn_w_gate, L1_ffn_w_up, L1_ffn_w_down):

    def _L0_attn_ref(emb, Wa_w, Wa_b, Wb_w, Wb_b, C_w, C_b, D_w, D_b, Wout_w, Wout_b, hn_g, hn_b, head_w, ffn1_w, ffn1_b, ffn2_w, ffn2_b, proj_w, proj_b, norm_g, norm_b):
        import jax, jax.numpy as jnp
        import numpy as np
        B, L, E, D, H = (2, 256, 128, 128, 8)

        def _ln(x, g, b, eps=1e-05):
            m = jnp.mean(x, axis=-1, keepdims=True)
            v = jnp.mean((x - m) ** 2, axis=-1, keepdims=True)
            return (x - m) * jax.lax.rsqrt(v + eps) * g + b
        nH = head_w.shape[0]
        a = jnp.tanh(jnp.einsum('ble,hde->blhd', emb, Wa_w) + Wa_b)
        bg = jnp.einsum('ble,hde->blhd', emb, Wb_w) + Wb_b
        aT = jnp.moveaxis(a, 1, 0)
        bT = jnp.moveaxis(bg, 1, 0)

        def step(h, ab):
            at, bt = ab
            h = at * h + bt
            return (h, h)
        h0 = jnp.zeros_like(aT[0])
        _, hs = jax.lax.scan(step, h0, (aT, bT))
        hs = jnp.moveaxis(hs, 0, 1)
        Dx = emb @ D_w.T + D_b
        out = (jnp.einsum('blhd,hkd->blhk', hs, C_w) + C_b) * Dx[:, :, None, :]
        out = _ln(out, hn_g, hn_b)
        sum_heads = (Dx + jnp.einsum('h,blhd->bld', head_w, out)) / nH
        z = sum_heads @ Wout_w.T + Wout_b
        u = z + _ln(z, norm_g, norm_b)
        ffn = jax.nn.gelu(u @ ffn1_w.T + ffn1_b, approximate=False)
        h_out = u + (ffn @ ffn2_w.T + ffn2_b)
        return h_out @ proj_w.T + proj_b

    def _L0_ffn_ref(hidden_states, W1, b1, W2, b2):
        import jax, jax.numpy as jnp
        import numpy as np
        HIDDEN = 128
        INTER = 512
        h = jax.nn.relu(jnp.einsum('bsh,hi->bsi', hidden_states, W1) + b1)
        return jnp.einsum('bsi,ih->bsh', h, W2) + b2

    def _L1_attn_ref(x, w_qkv, b_qkv, w_proj, b_proj):
        import jax, jax.numpy as jnp
        import numpy as np
        NUM_HEADS = 16
        B, N, C = x.shape
        H = NUM_HEADS
        D = C // H
        scale = D ** (-0.5)
        qkv = x @ w_qkv + b_qkv
        qkv = qkv.reshape(B, N, 3, H, D)
        q, k, v = (jnp.moveaxis(qkv, 2, 0)[i] for i in range(3))
        scores = jnp.einsum('bqhd,bkhd->bhqk', q.astype(jnp.float32), k.astype(jnp.float32)) * scale
        attn = jax.nn.softmax(scores, axis=-1).astype(q.dtype)
        out = jnp.einsum('bhqk,bkhd->bqhd', attn, v).reshape(B, N, C)
        return out @ w_proj + b_proj

    def _L1_ffn_ref(x, w_gate, w_up, w_down):
        import jax, jax.numpy as jnp
        import numpy as np
        DIM = 128
        HIDDEN = 384
        SCALE = 1.0 / 127.0

        def _dequant(w_int, dtype):
            return w_int.astype(dtype) * jnp.asarray(SCALE, dtype)
        wg = _dequant(w_gate, x.dtype)
        wu = _dequant(w_up, x.dtype)
        wd = _dequant(w_down, x.dtype)
        gate = jnp.einsum('bsd,hd->bsh', x, wg)
        up = jnp.einsum('bsd,hd->bsh', x, wu)
        h = jax.nn.silu(gate) * up
        return jnp.einsum('bsh,dh->bsd', h, wd)
    x = L0_attn_emb
    xn = _layernorm(x, axis=-1)
    x = x + _L0_attn_ref(xn, L0_attn_Wa_w, L0_attn_Wa_b, L0_attn_Wb_w, L0_attn_Wb_b, L0_attn_C_w, L0_attn_C_b, L0_attn_D_w, L0_attn_D_b, L0_attn_Wout_w, L0_attn_Wout_b, L0_attn_hn_g, L0_attn_hn_b, L0_attn_head_w, L0_attn_ffn1_w, L0_attn_ffn1_b, L0_attn_ffn2_w, L0_attn_ffn2_b, L0_attn_proj_w, L0_attn_proj_b, L0_attn_norm_g, L0_attn_norm_b) + _L0_ffn_ref(xn, L0_ffn_W1, L0_ffn_b1, L0_ffn_W2, L0_ffn_b2)
    xn = _layernorm(x, axis=-1)
    x = x + _L1_attn_ref(xn, L1_attn_w_qkv, L1_attn_b_qkv, L1_attn_w_proj, L1_attn_b_proj) + _L1_ffn_ref(xn, L1_ffn_w_gate, L1_ffn_w_up, L1_ffn_w_down)
    return x

_drawn_inputs = setup_inputs


def setup_inputs(seed=0):
    import zlib

    import numpy as np

    out = dict(_drawn_inputs(seed))
    spreads = {'L0_attn_Wa_b': (0.0, 0.8),
     'L0_attn_Wb_b': (0.0, 0.1),
     'L0_attn_C_b': (0.0, 0.1),
     'L0_attn_D_b': (0.0, 0.1),
     'L0_attn_Wout_b': (0.0, 0.1),
     'L0_attn_hn_g': (1.0, 0.2),
     'L0_attn_hn_b': (0.0, 0.38),
     'L0_attn_head_w': (1.0, 0.6),
     'L0_attn_ffn1_b': (0.0, 0.8),
     'L0_attn_ffn2_b': (0.0, 0.318),
     'L0_attn_proj_b': (0.0, 0.1),
     'L0_attn_norm_g': (1.0, 0.2),
     'L0_attn_norm_b': (0.0, 0.279),
     'L1_attn_b_qkv': (0.0, 2.0),
     'L1_attn_b_proj': (0.0, 2.0)}
    factors = {'L0_attn_Wa_w': 2.989,
     'L0_attn_ffn1_w': 3.984,
     'L0_attn_ffn2_w': 3.55,
     'L0_ffn_b1': 3.672,
     'L1_attn_w_qkv': 64.0,
     'L1_attn_w_proj': 58.432}
    for name, (base, spread) in spreads.items():
        noise = np.random.default_rng([zlib.crc32(name.encode()), seed]).standard_normal(out[name].shape)
        drawn = base * np.exp(spread * noise) if base else spread * noise
        out[name] = jnp.asarray(drawn.astype(out[name].dtype))
    for name, factor in factors.items():
        out[name] = (out[name] * factor).astype(out[name].dtype)
    return out
```

```python
from contextlib import ExitStack

import numpy as np

import concourse.bass as bass
from concourse import mybir

F32 = mybir.dt.float32
F32R = mybir.dt.float32r
I32 = mybir.dt.int32
ALU = mybir.AluOpType
ACT = mybir.ActivationFunctionType
AX = mybir.AxisListType

P = 128
ROWS = 8
L = 512
TT = L // P
NH = 8
FC = 4
GC = 3
HD = 8
AG = 4
SLOTS = 4 * AG * TT
EPS = 1e-5
DEQUANT = float(np.float32(1.0 / 127.0))
SM_SCALE = HD ** -0.5
POOL_CONST = 9
WEIGH_SLOT = 1
ATT_SLOT = 4
S_AHEAD = 22

W_COLS = {}
_at = 0
for _name, _n in (("wa", NH * P), ("wb", NH * P), ("c", NH * P), ("d", P), ("wout", P), ("f1", FC * P),
                  ("f2", FC * P), ("proj", P), ("r1", FC * P), ("r2", FC * P), ("qkv", 3 * P), ("ap", P)):
    W_COLS[_name] = _at
    _at += _n
W_TOTAL = _at
B_COLS = {}
_at = 0
for _name, _n in (("wa", NH), ("wb", NH), ("f1", FC), ("f2", 1), ("r1", FC), ("q", 1), ("k", 1)):
    B_COLS[_name] = _at
    _at += _n
B_TOTAL = _at
R_COLS = {}
_at = 0
for _name, _n in (("d", P), ("wout", P), ("ng", P), ("nb", P), ("proj", P), ("r2", P), ("v", P), ("ap", P),
                  ("hw", NH), ("hng", NH * P), ("hnb", NH * P)):
    R_COLS[_name] = _at
    _at += _n
R_TOTAL = _at
R_KEEP = R_COLS["hw"]


class Signal:

    def __init__(self, sem, per_row):
        self.sem, self.per_row = sem, per_row

    def of(self, row, n):
        return row * self.per_row + n


def two_block_model(nc, x, w_pack, wi_pack, b_pack, r_pack, cb, out):
    with ExitStack() as ctx:
        def sb(name, shape, dt=F32):
            return ctx.enter_context(nc.sbuf_tensor(name, shape, dt))

        def sig(name, per_row=1):
            return Signal(ctx.enter_context(nc.semaphore(name)), per_row)

        w = sb("w", [P, W_TOTAL])
        bias = sb("bias", [P, B_TOTAL])
        rowv = sb("rowv", [P, R_KEEP])
        wdq = sb("wdq", [P, 3 * GC * P])
        hw_g = sb("hw_g", [P, NH * P])
        hw_b = sb("hw_b", [P, P])
        pb2 = sb("pb2", [P, P])
        ident = sb("ident", [P, P])
        cb_split = sb("cb_split", [2, NH * P], F32R)
        cb_mask = sb("cb_mask", [2, 1])
        ones2 = sb("ones2", [2, P], F32R)
        neg_half = sb("neg_half", [P, TT * NH])
        zeros = sb("zeros", [32, L])

        xin = sb("xin", [P, TT, P])
        x_bias = sb("x_bias", [P, TT, P])
        xn = sb("xn", [P, TT, P])
        ln1 = sb("ln1", [P, TT, 10])
        xnT = sb("xnT", [P, L])
        decay = sb("decay", [P, 2, L])
        drive = sb("drive", [P, 2, L])
        hs = sb("hs", [P, NH, L])
        dx = sb("dx", [P, TT, P])
        dx_b = sb("dx_b", [P, TT, P])
        relu = sb("relu", [P, FC, L])
        prod = sb("prod", [P, TT, NH, P])
        hst = sb("hst", [P, TT * NH, 6])
        hv = sb("hv", [P, 8, TT * NH])
        hsum = sb("hsum", [P, TT, P])
        z = sb("z", [P, TT, P])
        lnz = sb("lnz", [P, TT, 10])
        zn = sb("zn", [P, TT, P])
        z_b = sb("z_b", [P, TT, P])
        uT = sb("uT", [P, L])
        shT = uT
        gel = sb("gel", [P, FC, L])
        hT = sb("hT", [P, L])
        x1 = sb("x1", [P, TT, P])

        x1_b = sb("x1_b", [P, TT, P])
        ln2 = sb("ln2", [P, TT, 10])
        xm = sb("xm", [P, TT, P])
        xmT = sb("xmT", [P, L])
        q_hi = sb("q_hi", [P, L], F32R)
        q_lo = sb("q_lo", [P, L], F32R)
        k_hi = sb("k_hi", [P, L], F32R)
        k_lo = sb("k_lo", [P, L], F32R)
        q_st = sb("q_st", [P, AG, L], F32R)
        k_st = sb("k_st", [P, AG, L], F32R)
        mx = sb("mx", [P, AG, TT, 4])
        m_hi = sb("m_hi", [4, L], F32R)
        m_lo = sb("m_lo", [4, L], F32R)
        vv = sb("vv", [P, TT, AG * 4, 32])
        prob = sb("prob", [P, 2, 4, L])
        oT = sb("oT", [P, L])
        rden = sb("rden", [P, TT, 4])
        att = sb("att", [P, TT, P])
        attT = oT
        g_tanh = sb("g_tanh", [P, L])
        ffh = sb("ffh", [P, GC, L])
        res = sb("res", [P, TT, P])
        res_held = sb("res_held", [P, TT, P])
        y = sb("y", [P, TT, P])

        r_tmp = prod[:, 0:3, :, :].rearrange("p t h k -> p (t h k)")
        cb_raw = prod[0:2, 3, :, :].rearrange("p h k -> p (h k)")
        cb_hi = hs[0:2, 0:2, :].rearrange("p h n -> p (h n)").bitcast(F32R)
        ones_row = relu[0:4, :, :]
        wi = prob[:, :, :, :].rearrange("p a b n -> p (a b n)").bitcast(I32)

        ps0 = ctx.enter_context(nc.psum_tensor("ps0", [P, 2, L], F32))
        ps_s = ctx.enter_context(nc.psum_tensor("ps_s", [P, 2, L], F32))
        ps_st = ctx.enter_context(nc.psum_tensor("ps_st", [P, 2, L], F32))
        ps_pv = ctx.enter_context(nc.psum_tensor("ps_pv", [P, L], F32))
        ps_c = ctx.enter_context(nc.psum_tensor("ps_c", [P, L], F32))

        w_loaded, wi_loaded, b_loaded, r_loaded, cb_loaded = (
            sig(n) for n in ("w_loaded", "wi_loaded", "b_loaded", "r_loaded", "cb_loaded"))
        pool_const, k_ones, su, const_ready = (sig(n) for n in ("pool_const", "k_ones", "su", "const_ready"))

        x_loaded = sig("x_loaded", 16)
        ln1_stats, ln1_var, ln1_veps, ln1_rstd = sig("ln1_stats", 4), sig("ln1_var", 4), sig("ln1_veps"), sig("ln1_rstd")
        xn_done, xnT_ps, xnT_done = sig("xn_done", TT), sig("xnT_ps"), sig("xnT_done")
        x_bias_done = sig("x_bias_done")
        rec_ps, decay_done, drive_done, scan_done = sig("rec_ps", 2 * NH), sig("decay_done", NH), sig("drive_done", NH), sig("scan_done", NH)
        dx_ps, dx_done, dx_b_done = sig("dx_ps"), sig("dx_done"), sig("dx_b_done", 2)
        relu_ps, relu_done = sig("relu_ps", FC), sig("relu_done", FC)
        head_ps, prod_done, head_stats, head_var, head_rstd = sig("head_ps", 2 * TT), sig("prod_done", 2 * TT), sig("head_stats", 2 * TT), sig("head_var", 14), sig("head_rstd", 2)
        head_shift = sig("head_shift", 2)
        head_norm, head_scaled, head_added, sum_done = sig("head_norm", TT), sig("head_scaled", TT), sig("head_added", TT), sig("sum_done")
        shT_ps, shT_done, z_ps, z_done, z_b_done = sig("shT_ps"), sig("shT_done"), sig("z_ps"), sig("z_done"), sig("z_b_done")
        lnz_stats, lnz_var, lnz_veps, lnz_rstd = sig("lnz_stats", 4), sig("lnz_var", 4), sig("lnz_veps"), sig("lnz_rstd")
        zn_done, zg_done, u_done, uT_ps, uT_done = sig("zn_done", TT), sig("zg_done"), sig("u_done"), sig("uT_ps"), sig("uT_done")
        f1_ps, gelu_done, f2_ps, hT_done, x1_ps, x1_done = sig("f1_ps", FC), sig("gelu_done", FC), sig("f2_ps"), sig("hT_done"), sig("x1_ps", TT), sig("x1_done")
        ln2_stats, ln2_var, ln2_veps, ln2_rstd = sig("ln2_stats", 4), sig("ln2_var", 4), sig("ln2_veps"), sig("ln2_rstd")
        xm_done, xmT_ps, xmT_done = sig("xm_done", TT), sig("xmT_ps"), sig("xmT_done")
        x1_b_done = sig("x1_b_done")
        qk_ps, qk_hi, qk_lo = sig("qk_ps", 2), sig("qk_hi", 2), sig("qk_lo", 2)
        stacked = [sig(f"stacked{g}", 16 * 7) for g in range(AG)]
        s_ps, s_max = sig("s_ps", SLOTS), sig("s_max", SLOTS)
        m_ps, m_hi_done, m_lo_done = sig("m_ps", AG), sig("m_hi_done", AG), sig("m_lo_done", AG)
        m_placed = [sig(f"m_placed{g}", 32) for g in range(AG)]
        v_ps, v_done = sig("v_ps"), sig("v_done")
        st_ps, exp_done, pv_done = sig("st_ps", SLOTS), sig("exp_done", SLOTS), sig("pv_done", AG * TT)
        oT_done, o_ps, rden_done, att_done = sig("oT_done", AG), sig("o_ps", AG), sig("rden_done", AG), sig("att_done", AG)
        gate_ps, tanh_done, g_lin_done, up_ps, ffh_done = sig("gate_ps", GC), sig("tanh_done", GC), sig("g_lin_done", GC), sig("up_ps", GC), sig("ffh_done", GC)
        res_ps, res_done, res_held_done = sig("res_ps"), sig("res_done"), sig("res_held_done")
        attT_ps, attT_done, y_ps, y_done, stored = sig("attT_ps"), sig("attT_done"), sig("y_ps"), sig("y_done"), sig("stored", 16)

        def has_past(row):
            return not (isinstance(row, int) and row < 1)

        def wcol(name, i=0, n=P):
            return w[:, W_COLS[name] + i * P:W_COLS[name] + i * P + n]

        def bcol(name, i=0):
            return bias[:, B_COLS[name] + i:B_COLS[name] + i + 1]

        def along(name):
            return rowv[:, R_COLS[name]:R_COLS[name] + P].unsqueeze(1).to_broadcast([P, TT, P])

        def flat(t):
            return t[:, :, :].rearrange("p t n -> p (t n)")

        beside = {
            0: "stack3 a, shT c, ln1 n", 1: "values a", 2: "z c, xn n", 3: "xnT n",
            4: "att3 t, lnz c, rec0 n", 5: "attT t, rec1 n", 6: "u c", 7: "store t, rec2 n", 8: "rec3 n",
            9: "uT c", 10: "rec4 n, hold a", 11: "ffn1_0 c, rec5 n", 13: "ffn1_1 c, rec6 n",
            14: "rec7 n", 15: "ffn1_2 c", 16: "rec8 n", 17: "ffn1_3 c, rec9 n", 19: "ffn2 c, rec10 n",
            20: "att0 a, rec11 n", 21: "x1_0 c", 22: "x1_1 c, rec12 n", 23: "x1_2 c, rec13 n", 24: "x1_3 c",
            25: "ln2 c, x_bias n, rec14 n", 26: "rec15 n", 28: "xm c, dx n", 30: "xmT c, head0 n",
            32: "query c, head1 n", 33: "load f", 34: "key c", 35: "stack0 c, head2 n",
            36: "att1 a, stack1 c", 37: "head3 n", 38: "norm0 n, gate0 c", 40: "head4 n, up0 c", 42: "head5 n", 43: "gate1 c",
            44: "head6 n, stack2 c", 45: "up1 c", 46: "head7 n", 47: "norm1 n", 48: "gate2 c", 50: "relu0 n, up2 c",
            51: "relu1 n", 52: "att2 a, sum0 n", 54: "res c, sum1 n", 56: "relu2 n", 58: "relu3 n, sum2 n",
            62: "sum3 n",
        }
        for g in range(AG):
            k = 16 * (g + 1) - S_AHEAD
            at = k % SLOTS
            beside[at] = f"max{g} " + ("c" if k < 0 else "a") + (", " + beside[at] if at in beside else "")

        offset = {"t": -2, "a": -1, "c": 0, "n": 1, "f": 2}

        def step(i, lo, hi, attention, pieces):
            rows = {who: i + off for who, off in offset.items() if 0 <= lo + off and hi + off < ROWS}
            for slot in range(SLOTS):
                attention(slot, rows)
                for item in beside.get(slot, "").split(", "):
                    name, _, who = item.partition(" ")
                    if who in rows and name in pieces:
                        pieces[name](rows[who], rows)

        def pipeline(eng, attention, pieces):
            first, last = 3, ROWS - 3
            for i in range(-1, first):
                step(i, i, i, attention, pieces)
            with eng.Fori(first, last + 1) as i:
                step(i, first, last, attention, pieces)
            for i in range(last + 1, ROWS + 2):
                step(i, i, i, attention, pieces)

        block = ctx.enter_context(nc.Block())

        @block.sync
        def _(sp):
            sp.dma_start(w[:, :], w_pack).then_inc(w_loaded.sem, 16)
            sp.dma_start(bias[:, :], b_pack).then_inc(b_loaded.sem, 16)
            sp.dma_start(rowv[:, :], r_pack[:, 0:R_KEEP].to_broadcast([P, R_KEEP])).then_inc(r_loaded.sem, 16)
            sp.dma_start(r_tmp[:, 0:R_TOTAL - R_KEEP],
                         r_pack[:, R_KEEP:].to_broadcast([P, R_TOTAL - R_KEEP])).then_inc(r_loaded.sem, 16)
            sp.dma_start(wi[:, 0:3 * GC * P], wi_pack).then_inc(wi_loaded.sem, 16)
            sp.dma_start(cb_raw, cb.to_broadcast([2, NH * P])).then_inc(cb_loaded.sem, 16)
            sp.wait_ge(pool_const.sem, POOL_CONST)
            for d in range(2):
                sp.dma_start(k_st[4 * d + 3:4 * d + 3 + 97:32, :, :].bitcast(F32),
                             ones_row).then_inc(k_ones.sem, 16)

            x_rows = x.rearrange("(b t p) e -> b p t e", b=ROWS, t=TT)
            out_rows = out.rearrange("(b t p) e -> b p t e", b=ROWS, t=TT)

            sp.dma_start(xin[:, :, :], x_rows[0]).then_inc(x_loaded.sem, 16)

            def load(r, rows):
                if has_past(r):
                    sp.wait_ge(x_bias_done.sem, x_bias_done.of(r - 1, 1))
                sp.dma_start(xin[:, :, :], x_rows[r]).then_inc(x_loaded.sem, 16)

            def stack(g):
                def piece(r, rows):
                    if g == 0:
                        sp.wait_ge(qk_lo.sem, qk_lo.of(r, 2))
                    if has_past(r):
                        sp.wait_ge(st_ps.sem, st_ps.of(r - 1, 16 * (g + 1)))
                    half = slice(32 * g, 32 * g + 32)
                    for j, (kp, qp) in enumerate(((k_hi, q_hi), (k_hi, q_lo), (k_lo, q_hi))):
                        for st, part in ((k_st, kp), (q_st, qp)):
                            sp.dma_start(st[j:j + 125:4, g, :].bitcast(F32),
                                         part[half, :].bitcast(F32)).then_inc(stacked[g].sem, 16)
                    sp.dma_start(q_st[3:3 + 125:4, g, :].bitcast(F32), zeros[:, :]).then_inc(stacked[g].sem, 16)
                return piece

            def place_max(g):
                def piece(r, rows):
                    sp.wait_ge(m_lo_done.sem, m_lo_done.of(r, g + 1))
                    for d, part in enumerate((m_hi, m_lo)):
                        sp.dma_start(q_st[4 * d + 3:4 * d + 3 + 97:32, g, :].bitcast(F32),
                                     part[:, :].bitcast(F32)).then_inc(m_placed[g].sem, 16)
                return piece

            def store(r, rows):
                sp.wait_ge(y_done.sem, y_done.of(r, 1))
                sp.dma_start(out_rows[r], y[:, :, :]).then_inc(stored.sem, 16)

            pieces = {"load": load, "store": store}
            for g in range(AG):
                pieces[f"stack{g}"] = stack(g)
                pieces[f"max{g}"] = place_max(g)
            pipeline(sp, lambda slot, rows: None, pieces)
            sp.wait_ge(stored.sem, 16 * ROWS)

        @block.tensor
        def _(pe):
            pe.wait_ge(w_loaded.sem, 16)
            pe.wait_ge(const_ready.sem, 1)
            pe.wait_ge(k_ones.sem, 32)


            def transposes(bank, src, signal):
                for t in range(TT):
                    mm = pe.transpose(bank[:, t * P:(t + 1) * P], src[:, t, :], ident[:, :])
                mm.then_inc(signal.sem, 1)

            def xnT_(r, rows):
                pe.wait_ge(xn_done.sem, xn_done.of(r, TT))
                if has_past(r):
                    pe.wait_ge(relu_done.sem, relu_done.of(r - 1, FC - 1))
                transposes(ps0[:, 0, :], xn, xnT_ps)

            def rec(k):
                h = k // 2

                def decay_(r, rows):
                    pe.wait_ge(xnT_done.sem, xnT_done.of(r, 1))
                    if h:
                        pe.wait_ge(decay_done.sem, decay_done.of(r, h))
                    elif has_past(r):
                        pe.wait_ge(relu_done.sem, relu_done.of(r - 1, FC))
                    pe.matmul(ps0[:, 1, :], wcol("wa", h), xnT[:, :], start=True, stop=True).then_inc(rec_ps.sem, 1)

                def drive_(r, rows):
                    if h:
                        pe.wait_ge(drive_done.sem, drive_done.of(r, h))
                    pe.matmul(ps0[:, 0, :], wcol("wb", h), xnT[:, :], start=True, stop=True).then_inc(rec_ps.sem, 1)
                return drive_ if k % 2 else decay_

            def dx_(r, rows):
                pe.wait_ge(decay_done.sem, decay_done.of(r, NH))
                for t in range(TT):
                    mm = pe.matmul(ps0[:, 1, t * P:(t + 1) * P], xnT[:, t * P:(t + 1) * P], wcol("d"),
                                   start=True, stop=True)
                mm.then_inc(dx_ps.sem, 1)

            def head(k):
                t, half = divmod(k, 2)

                def piece(r, rows):
                    if k == 0:
                        pe.wait_ge(scan_done.sem, scan_done.of(r, NH))
                        pe.wait_ge(drive_done.sem, drive_done.of(r, NH))
                    elif k == 1:
                        pe.wait_ge(dx_done.sem, dx_done.of(r, 1))
                    else:
                        pe.wait_ge(prod_done.sem, prod_done.of(r, k - 1))
                    bank = ps0[:, half, :]
                    pe.matmul(bank, ones2[:, :], cb_split[:, half * L:(half + 1) * L], start=True, stop=False,
                              skip_group_check=True)
                    for h in range(4):
                        mm = pe.matmul(bank[:, h * P:(h + 1) * P], hs[:, 4 * half + h, t * P:(t + 1) * P],
                                       wcol("c", 4 * half + h), start=False, stop=(h == 3),
                                       skip_group_check=True)
                    mm.then_inc(head_ps.sem, 1)
                return piece

            def relu_(j):
                def piece(r, rows):
                    if j < 2:
                        pe.wait_ge(prod_done.sem, prod_done.of(r, 2 * TT - 1 + j))
                    else:
                        pe.wait_ge(relu_done.sem, relu_done.of(r, j - 1))
                    pe.matmul(ps0[:, j % 2, :], wcol("r1", j), xnT[:, :], start=True, stop=True)\
                        .then_inc(relu_ps.sem, 1)
                return piece

            def shT_(r, rows):
                pe.wait_ge(sum_done.sem, sum_done.of(r, 1))
                if has_past(r):
                    pe.wait_ge(res_done.sem, res_done.of(r - 1, 1))
                transposes(ps_c[:, :], hsum, shT_ps)

            def values(r, rows):
                pe.wait_ge(res_done.sem, res_done.of(r, 1))
                if "c" in rows:
                    pe.wait_ge(shT_done.sem, shT_done.of(rows["c"], 1))
                for t in range(TT):
                    mm = pe.matmul(ps_c[:, t * P:(t + 1) * P], xmT[:, t * P:(t + 1) * P], wcol("qkv", 2),
                                   start=True, stop=True)
                mm.then_inc(v_ps.sem, 1)

            def z_(r, rows):
                pe.wait_ge(shT_done.sem, shT_done.of(r, 1))
                if "a" in rows:
                    pe.wait_ge(v_done.sem, v_done.of(rows["a"], 1))
                for t in range(TT):
                    mm = pe.matmul(ps_c[:, t * P:(t + 1) * P], shT[:, t * P:(t + 1) * P], wcol("wout"),
                                   start=True, stop=True)
                mm.then_inc(z_ps.sem, 1)

            def attT_(r, rows):
                pe.wait_ge(att_done.sem, att_done.of(r, AG))
                if "c" in rows:
                    pe.wait_ge(z_done.sem, z_done.of(rows["c"], 1))
                elif "a" in rows:
                    pe.wait_ge(v_done.sem, v_done.of(rows["a"], 1))
                transposes(ps_c[:, :], att, attT_ps)

            def store(r, rows):
                pe.wait_ge(attT_done.sem, attT_done.of(r, 1))
                for t in range(TT):
                    mm = pe.matmul(ps_c[:, t * P:(t + 1) * P], attT[:, t * P:(t + 1) * P], wcol("ap"),
                                   start=True, stop=True)
                mm.then_inc(y_ps.sem, 1)

            def uT_(r, rows):
                pe.wait_ge(u_done.sem, u_done.of(r, 1))
                if "t" in rows:
                    pe.wait_ge(y_done.sem, y_done.of(rows["t"], 1))
                transposes(ps_c[:, :], zn, uT_ps)

            def ffn1(j):
                def piece(r, rows):
                    if j == 0:
                        pe.wait_ge(uT_done.sem, uT_done.of(r, 1))
                    else:
                        pe.wait_ge(gelu_done.sem, gelu_done.of(r, j))
                    pe.matmul(ps_c[:, :], wcol("f1", j), uT[:, :], start=True, stop=True).then_inc(f1_ps.sem, 1)
                return piece

            def ffn2(r, rows):
                pe.wait_ge(gelu_done.sem, gelu_done.of(r, FC))
                for j in range(FC):
                    mm = pe.matmul(ps_c[:, :], wcol("f2", j), gel[:, j, :], start=(j == 0), stop=(j == FC - 1))
                mm.then_inc(f2_ps.sem, 1)

            def x1_(t):
                def piece(r, rows):
                    if t == 0:
                        pe.wait_ge(relu_done.sem, relu_done.of(r, FC))
                        pe.wait_ge(hT_done.sem, hT_done.of(r, 1))
                    cols = slice(t * P, (t + 1) * P)
                    for j in range(FC):
                        pe.matmul(ps_c[:, cols], relu[:, j, cols], wcol("r2", j), start=(j == 0), stop=False)
                    pe.matmul(ps_c[:, cols], hT[:, cols], wcol("proj"), start=False, stop=True).then_inc(x1_ps.sem, 1)
                return piece

            def xmT_(r, rows):
                pe.wait_ge(xm_done.sem, xm_done.of(r, TT))
                transposes(ps_c[:, :], xm, xmT_ps)

            def query(r, rows):
                pe.wait_ge(xmT_done.sem, xmT_done.of(r, 1))
                pe.matmul(ps_c[:, :], wcol("qkv", 0), xmT[:, :], start=True, stop=True).then_inc(qk_ps.sem, 1)

            def key(r, rows):
                pe.wait_ge(qk_lo.sem, qk_lo.of(r, 1))
                pe.matmul(ps_c[:, :], wcol("qkv", 1), xmT[:, :], start=True, stop=True).then_inc(qk_ps.sem, 1)

            def gate(j):
                def piece(r, rows):
                    if j == 0:
                        pe.wait_ge(qk_lo.sem, qk_lo.of(r, 2))
                    else:
                        pe.wait_ge(ffh_done.sem, ffh_done.of(r, j))
                    pe.matmul(ps_c[:, :], wdq[:, j * P:(j + 1) * P], xmT[:, :], start=True, stop=True)\
                        .then_inc(gate_ps.sem, 1)
                return piece

            def up(j):
                def piece(r, rows):
                    pe.wait_ge(g_lin_done.sem, g_lin_done.of(r, j + 1))
                    pe.matmul(ps_c[:, :], wdq[:, (GC + j) * P:(GC + j + 1) * P], xmT[:, :], start=True, stop=True)\
                        .then_inc(up_ps.sem, 1)
                return piece

            def res_(r, rows):
                pe.wait_ge(ffh_done.sem, ffh_done.of(r, GC))
                for t in range(TT):
                    for j in range(GC):
                        mm = pe.matmul(ps_c[:, t * P:(t + 1) * P], ffh[:, j, t * P:(t + 1) * P],
                                       wdq[:, (2 * GC + j) * P:(2 * GC + j + 1) * P],
                                       start=(j == 0), stop=(j == GC - 1))
                mm.then_inc(res_ps.sem, 1)

            def turn_max(g):
                def piece(r, rows):
                    pe.wait_ge(s_max.sem, s_max.of(r, 16 * (g + 1)))
                    for t in range(TT):
                        mm = pe.transpose(ps_s[0:4, 1, t * P:(t + 1) * P], mx[:, g, t, :], ident[:, :])
                    mm.then_inc(m_ps.sem, 1)
                return piece

            def turn_att(g):
                def piece(r, rows):
                    pe.wait_ge(oT_done.sem, oT_done.of(r, g + 1))
                    k = ATT_SLOT + 16 * (g + 1)
                    if g < AG - 1:
                        pe.wait_ge(exp_done.sem, exp_done.of(r, k))
                    elif "a" in rows:
                        pe.wait_ge(exp_done.sem, exp_done.of(r + 1, k - SLOTS))
                    for t in range(TT):
                        mm = pe.transpose(ps_st[:, 1, t * P:(t + 1) * P], oT[:, t * P:(t + 1) * P], ident[:, :])
                    mm.then_inc(o_ps.sem, 1)
                return piece

            def scores(r, n):
                g, qt, h = n // 16, n // 4 % TT, n % 4
                if n % 16 == 0:
                    pe.wait_ge(stacked[g].sem, stacked[g].of(r, 16 * 7))
                if n == 1 and has_past(r):
                    pe.wait_ge(m_lo_done.sem, m_lo_done.of(r - 1, AG))
                elif n % 16 == 1 and n > 1:
                    pe.wait_ge(m_lo_done.sem, m_lo_done.of(r, g))
                elif n >= 2:
                    pe.wait_ge(s_max.sem, s_max.of(r, n - 1))
                elif has_past(r):
                    pe.wait_ge(s_max.sem, s_max.of(r - 1, SLOTS - 1))
                part = slice(32 * h, 32 * h + 32)
                pe.matmul(ps_s[:, n % 2, :], q_st[part, g, qt * P:(qt + 1) * P], k_st[part, g, :],
                          start=True, stop=True).then_inc(s_ps.sem, 1)

            def scores_t(r, n, rows):
                g, kt, h = n // 16, n // 4 % TT, n % 4
                if n % 16 == 0:
                    pe.wait_ge(m_placed[g].sem, m_placed[g].of(r, 32))
                if n == ATT_SLOT + 1 and "t" in rows:
                    pe.wait_ge(att_done.sem, att_done.of(rows["t"], AG))
                elif n > 16 and n % 16 == ATT_SLOT + 1:
                    pe.wait_ge(att_done.sem, att_done.of(r, g))
                elif n >= 2:
                    pe.wait_ge(exp_done.sem, exp_done.of(r, n - 1))
                elif has_past(r):
                    pe.wait_ge(exp_done.sem, exp_done.of(r - 1, SLOTS - 1 + n))
                part = slice(32 * h, 32 * h + 32)
                pe.matmul(ps_st[:, n % 2, :], k_st[part, g, kt * P:(kt + 1) * P], q_st[part, g, :],
                          start=True, stop=True).then_inc(st_ps.sem, 1)

            def weigh(r, u):
                g, kt = divmod(u, TT)
                pe.wait_ge(exp_done.sem, exp_done.of(r, 4 * u + 4))
                if u == 0:
                    pe.wait_ge(v_done.sem, v_done.of(r, 1))
                if kt == 0:
                    if g:
                        pe.wait_ge(oT_done.sem, oT_done.of(r, g))
                    elif has_past(r):
                        pe.wait_ge(oT_done.sem, oT_done.of(r - 1, AG))
                for h in range(4):
                    mm = pe.matmul(ps_pv[32 * h:32 * h + 32, :], vv[:, kt, 4 * g + h, :], prob[:, u % 2, h, :],
                                   start=(kt == 0), stop=(kt == TT - 1))
                mm.then_inc(pv_done.sem, 1)

            def attention(slot, rows):
                if "a" in rows:
                    scores_t(rows["a"], slot, rows)
                n = slot + S_AHEAD
                if n < SLOTS and "a" in rows:
                    scores(rows["a"], n)
                if n >= SLOTS and "c" in rows:
                    scores(rows["c"], n - SLOTS)
                if slot == WEIGH_SLOT and "t" in rows:
                    weigh(rows["t"], SLOTS // 4 - 1)
                if slot > 4 and slot % 4 == WEIGH_SLOT and "a" in rows:
                    weigh(rows["a"], slot // 4 - 1)

            pieces = {"xn": xnT_, "dx": dx_, "shT": shT_, "z": z_, "uT": uT_, "ffn2": ffn2, "xmT": xmT_,
                      "query": query, "key": key, "values": values, "res": res_, "attT": attT_, "store": store}
            for k in range(2 * NH):
                pieces[f"rec{k}"] = rec(k)
                pieces[f"head{k // 2}"] = head(k // 2)
            for k in range(4):
                pieces[f"relu{k}"] = relu_(k)
                pieces[f"ffn1_{k}"] = ffn1(k)
                pieces[f"x1_{k}"] = x1_(k)
                pieces[f"max{k}"] = turn_max(k)
                pieces[f"att{k}"] = turn_att(k)
            for j in range(GC):
                pieces[f"gate{j}"] = gate(j)
                pieces[f"up{j}"] = up(j)
            pipeline(pe, attention, pieces)


        @block.scalar
        def _(act):
            act.wait_ge(b_loaded.sem, 16)

            def copy_out(dst, src, ps, done):
                def piece(r, rows):
                    act.wait_ge(ps.sem, ps.of(r, 1))
                    act.activation(dst, src, ACT.Copy).then_inc(done.sem, 1)
                return piece

            def rec(k):
                h = k // 2

                def decay_(r, rows):
                    act.wait_ge(rec_ps.sem, rec_ps.of(r, k + 1))
                    if h >= 2:
                        act.wait_ge(scan_done.sem, scan_done.of(r, h - 1))
                    act.activation(decay[:, h % 2, :], ps0[:, 1, :], ACT.Tanh, bias=bcol("wa", h))\
                        .then_inc(decay_done.sem, 1)

                def drive_(r, rows):
                    act.wait_ge(rec_ps.sem, rec_ps.of(r, k + 1))
                    act.activation(drive[:, h % 2, :], ps0[:, 0, :], ACT.Identity, bias=bcol("wb", h))\
                        .then_inc(drive_done.sem, 1)
                return drive_ if k % 2 else decay_

            def relu_(j):
                def piece(r, rows):
                    act.wait_ge(relu_ps.sem, relu_ps.of(r, j + 1))
                    act.activation(relu[:, j, :], ps0[:, j % 2, :], ACT.Relu, bias=bcol("r1", j))\
                        .then_inc(relu_done.sem, 1)
                return piece

            def ffn1(j):
                def piece(r, rows):
                    act.wait_ge(f1_ps.sem, f1_ps.of(r, j + 1))
                    act.activation(gel[:, j, :], ps_c[:, :], ACT.Gelu, bias=bcol("f1", j)).then_inc(gelu_done.sem, 1)
                return piece

            def high(part, hi, name):
                def piece(r, rows):
                    act.wait_ge(qk_ps.sem, qk_ps.of(r, part + 1))
                    act.activation(hi[:, :], ps_c[:, :], ACT.Identity, bias=bcol(name)).then_inc(qk_hi.sem, 1)
                return piece

            def split_max(g):
                def piece(r, rows):
                    act.wait_ge(m_ps.sem, m_ps.of(r, g + 1))
                    act.activation(m_hi[:, :], ps_s[0:4, 1, :], ACT.Copy, scale=-1.0).then_inc(m_hi_done.sem, 1)
                return piece

            def gate(j):
                def piece(r, rows):
                    act.wait_ge(gate_ps.sem, gate_ps.of(r, j + 1))
                    act.activation(g_tanh[:, :], ps_c[:, :], ACT.Tanh, scale=0.5).then_inc(tanh_done.sem, 1)
                return piece

            def keep_weighed(r, g):
                act.wait_ge(pv_done.sem, pv_done.of(r, TT * (g + 1)))
                act.activation(oT[:, :], ps_pv[:, :], ACT.Copy).then_inc(oT_done.sem, 1)

            def attention(slot, rows):
                if "a" in rows:
                    r, buf, h = rows["a"], slot // 4 % 2, slot % 4
                    act.wait_ge(st_ps.sem, st_ps.of(r, slot + 1))
                    act.activation(prob[:, buf, h, :], ps_st[:, slot % 2, :], ACT.Exp, scale=SM_SCALE)\
                        .then_inc(exp_done.sem, 1)
                if slot == WEIGH_SLOT and "t" in rows:
                    keep_weighed(rows["t"], AG - 1)
                if slot > 16 and slot % 16 == WEIGH_SLOT and "a" in rows:
                    keep_weighed(rows["a"], slot // 16 - 1)

            pieces = {"xnT": copy_out(xnT[:, :], ps0[:, 0, :], xnT_ps, xnT_done),
                      "shT": copy_out(shT[:, :], ps_c[:, :], shT_ps, shT_done),
                      "uT": copy_out(uT[:, :], ps_c[:, :], uT_ps, uT_done),
                      "xmT": copy_out(xmT[:, :], ps_c[:, :], xmT_ps, xmT_done),
                      "attT": copy_out(attT[:, :], ps_c[:, :], attT_ps, attT_done),
                      "query": high(0, q_hi, "q"), "key": high(1, k_hi, "k")}
            for k in range(2 * NH):
                pieces[f"rec{k}"] = rec(k)
            for k in range(4):
                pieces[f"relu{k}"] = relu_(k)
                pieces[f"ffn1_{k}"] = ffn1(k)
            for j in range(GC):
                pieces[f"gate{j}"] = gate(j)
            for g in range(AG):
                pieces[f"max{g}"] = split_max(g)
            pipeline(act, attention, pieces)

        @block.vector
        def _(dve):
            made = [0]

            def chain(ins):
                made[0] += 1
                ins.then_inc(su.sem, 1)
                dve.wait_ge(su.sem, made[0])

            dve.memset(cb_mask[:, :], -1.0).then_inc(su.sem, 1)
            made[0] += 1
            dve.wait_ge(su.sem, made[0])
            chain(dve.memset(cb_mask[0:1, :], 0.0))
            chain(dve.memset(ones2[:, :].bitcast(F32), 1.0))
            dve.wait_ge(cb_loaded.sem, 16)
            chain(dve.tensor_copy(cb_hi, cb_raw))
            chain(dve.scalar_tensor_tensor(out=cb_split[:, :], in0=hs[0:2, 0:2, :].rearrange("p h n -> p (h n)"), scalar=cb_mask[:, 0:1],
                                           in1=cb_raw, op0=ALU.mult, op1=ALU.add))
            dve.wait_ge(wi_loaded.sem, 16)
            chain(dve.tensor_scalar(wdq[:, :], wi[:, 0:3 * GC * P], DEQUANT, None, ALU.mult))
            dve.wait_ge(r_loaded.sem, 32)
            chain(dve.tensor_tensor(pb2[:, :], rowv[:, R_COLS["proj"]:R_COLS["proj"] + P],
                                    rowv[:, R_COLS["r2"]:R_COLS["r2"] + P], ALU.add))
            hw8 = r_tmp[:, 0:NH]
            chain(dve.tensor_scalar(hw8, hw8, 1.0 / NH, None, ALU.mult))
            hw_all = hw8.unsqueeze(2).to_broadcast([P, NH, P])
            hng = r_tmp[:, NH:NH + NH * P].rearrange("p (h k) -> p h k", h=NH)
            hnb = r_tmp[:, NH + NH * P:NH + 2 * NH * P].rearrange("p (h k) -> p h k", h=NH)
            chain(dve.tensor_tensor(hw_g[:, :].rearrange("p (h k) -> p h k", h=NH), hng, hw_all, ALU.mult))
            chain(dve.tensor_tensor(hnb, hnb, hw_all, ALU.mult))
            chain(dve.tensor_reduce(hw_b[:, :], hnb.rearrange("p h k -> p k h"), AX.X, ALU.add))
            dve.wait_ge(pool_const.sem, POOL_CONST)
            dve.memset(hv[:, :, :], 0.0).then_inc(const_ready.sem, 1)

            def norm_stats(src, ready, ready_n, buf, stats, var, veps):
                def piece(r, rows):
                    dve.wait_ge(ready.sem, ready.of(r, ready_n))
                    for t in range(TT):
                        dve.bn_stats(buf[:, t, 0:6], src[:, t, :]).then_inc(stats.sem, 1)
                    dve.wait_ge(stats.sem, stats.of(r, TT))
                    dve.memset(buf[:, :, 8], EPS)
                    for t in range(TT):
                        dve.bn_aggr(buf[:, t, 6:8], buf[:, t, 0:6]).then_inc(var.sem, 1)
                    dve.wait_ge(var.sem, var.of(r, TT))
                    dve.tensor_tensor(buf[:, :, 8], buf[:, :, 7], buf[:, :, 8], ALU.add).then_inc(veps.sem, 1)
                return piece

            def normalise(dst, src, buf, rstd, done):
                def piece(r, rows):
                    dve.wait_ge(rstd.sem, rstd.of(r, 1))
                    for t in range(TT):
                        dve.tensor_scalar(dst[:, t, :], src[:, t, :], buf[:, t, 6:7], buf[:, t, 9:10],
                                          ALU.subtract, ALU.mult).then_inc(done.sem, 1)
                return piece

            def scan(h):
                def piece(r, rows):
                    dve.wait_ge(decay_done.sem, decay_done.of(r, h + 1))
                    dve.wait_ge(drive_done.sem, drive_done.of(r, h + 1))
                    dve.tensor_tensor_scan(hs[:, h, :], decay[:, h % 2, :], drive[:, h % 2, :], 0.0,
                                           ALU.mult, ALU.add).then_inc(scan_done.sem, 1)
                return piece

            def dx_(r, rows):
                dve.wait_ge(dx_ps.sem, dx_ps.of(r, 1))
                dve.tensor_tensor(dx[:, :, :], ps0[:, 1, :].rearrange("p (t k) -> p t k", t=TT), along("d"),
                                  ALU.add).then_inc(dx_done.sem, 1)

            def head_moments(r, k):
                dve.wait_ge(prod_done.sem, prod_done.of(r, k + 1))
                for h in range(4):
                    ins = dve.bn_stats(hst[:, 4 * k + h, :], prod[:, k // 2, 4 * (k % 2) + h, :])
                ins.then_inc(head_stats.sem, 1)

            def head(k):
                t, half = divmod(k, 2)

                def piece(r, rows):
                    if k == 0:
                        dve.wait_ge(dx_done.sem, dx_done.of(r, 1))
                    dve.wait_ge(head_ps.sem, head_ps.of(r, k + 1))
                    dve.tensor_tensor(prod[:, t, 4 * half:4 * half + 4, :],
                                      ps0[:, half, :].rearrange("p (h k) -> p h k", h=4),
                                      dx[:, t, :].unsqueeze(1).to_broadcast([P, 4, P]), ALU.mult)\
                        .then_inc(prod_done.sem, 1)
                    if k % 4:
                        head_moments(r, k - 1)
                return piece

            def norm(half):
                c = slice(half * TT * NH // 2, (half + 1) * TT * NH // 2)

                def piece(r, rows):
                    head_moments(r, 4 * half + 3)
                    dve.wait_ge(head_stats.sem, head_stats.of(r, 4 * half + 4))
                    dve.tensor_tensor(hv[:, 0, c], hst[:, c, 1], hst[:, c, 4], ALU.add).then_inc(head_var.sem, 1)
                    dve.tensor_tensor(hv[:, 1, c], hst[:, c, 1], hst[:, c, 4], ALU.subtract).then_inc(head_var.sem, 1)
                    dve.tensor_tensor(hv[:, 2, c], hst[:, c, 2], hst[:, c, 5], ALU.add).then_inc(head_var.sem, 1)
                    dve.wait_ge(head_var.sem, head_var.of(r, 7 * half + 3))
                    dve.tensor_scalar(hv[:, 7, c], hv[:, 0, c], -0.5, None, ALU.mult).then_inc(head_var.sem, 1)
                    dve.tensor_scalar(hv[:, 3, c], hv[:, 2, c], 1.0 / P, EPS, ALU.mult, ALU.add)\
                        .then_inc(head_var.sem, 1)
                    dve.scalar_tensor_tensor(out=hv[:, 4, c], in0=hv[:, 1, c], scalar=0.25, in1=hv[:, 1, c],
                                             op0=ALU.mult, op1=ALU.mult).then_inc(head_var.sem, 1)
                    dve.wait_ge(head_var.sem, head_var.of(r, 7 * half + 6))
                    dve.tensor_tensor(hv[:, 5, c], hv[:, 3, c], hv[:, 4, c], ALU.add).then_inc(head_var.sem, 1)
                return piece

            def sum_(t):
                def piece(r, rows):
                    dve.wait_ge(head_scaled.sem, head_scaled.of(r, t + 1))
                    dve.tensor_reduce(hsum[:, t, :], prod[:, t, :, :].rearrange("p h k -> p k h"), AX.X, ALU.add)\
                        .then_inc(head_added.sem, 1)
                    if t == TT - 1:
                        dve.wait_ge(head_added.sem, head_added.of(r, TT))
                        dve.wait_ge(dx_b_done.sem, dx_b_done.of(r, 2))
                        dve.tensor_tensor(hsum[:, :, :], hsum[:, :, :], dx_b[:, :, :], ALU.add).then_inc(sum_done.sem, 1)
                return piece

            def z_(r, rows):
                dve.wait_ge(z_ps.sem, z_ps.of(r, 1))
                dve.tensor_tensor(z[:, :, :], ps_c[:, :].rearrange("p (t k) -> p t k", t=TT), along("wout"),
                                  ALU.add).then_inc(z_done.sem, 1)

            def u_(r, rows):
                normalise(zn, z, lnz, lnz_rstd, zn_done)(r, rows)
                dve.wait_ge(zn_done.sem, zn_done.of(r, TT))
                dve.tensor_tensor(zn[:, :, :], zn[:, :, :], along("ng"), ALU.mult).then_inc(zg_done.sem, 1)
                dve.wait_ge(zg_done.sem, zg_done.of(r, 1))
                dve.wait_ge(z_b_done.sem, z_b_done.of(r, 1))
                dve.tensor_tensor(zn[:, :, :], zn[:, :, :], z_b[:, :, :], ALU.add).then_inc(u_done.sem, 1)

            def ffn2(r, rows):
                dve.wait_ge(f2_ps.sem, f2_ps.of(r, 1))
                dve.wait_ge(uT_done.sem, uT_done.of(r, 1))
                dve.scalar_tensor_tensor(out=hT[:, :], in0=ps_c[:, :], scalar=bcol("f2"), in1=uT[:, :],
                                         op0=ALU.add, op1=ALU.add).then_inc(hT_done.sem, 1)

            def x1_(r, rows):
                dve.wait_ge(x1_ps.sem, x1_ps.of(r, TT))
                dve.wait_ge(x_bias_done.sem, x_bias_done.of(r, 1))
                dve.tensor_tensor(flat(x1), ps_c[:, :], flat(x_bias), ALU.add).then_inc(x1_done.sem, 1)

            def low(part, hi, lo, name):
                def piece(r, rows):
                    dve.wait_ge(qk_hi.sem, qk_hi.of(r, part + 1))
                    dve.scalar_tensor_tensor(out=lo[:, :], in0=ps_c[:, :], scalar=bcol(name),
                                             in1=hi[:, :].bitcast(F32), op0=ALU.add, op1=ALU.subtract)\
                        .then_inc(qk_lo.sem, 1)
                return piece

            def split_max(g):
                def piece(r, rows):
                    dve.wait_ge(m_hi_done.sem, m_hi_done.of(r, g + 1))
                    dve.scalar_tensor_tensor(out=m_lo[:, :], in0=ps_s[0:4, 1, :], scalar=-1.0,
                                             in1=m_hi[:, :].bitcast(F32), op0=ALU.mult, op1=ALU.subtract)\
                        .then_inc(m_lo_done.sem, 1)
                return piece

            def values(r, rows):
                dve.wait_ge(v_ps.sem, v_ps.of(r, 1))
                b = rowv[:, R_COLS["v"]:R_COLS["v"] + P].rearrange("p (h d) -> p h d", d=HD).unsqueeze(1)
                dve.tensor_tensor(vv[:, :, :, 0:HD], ps_c[:, :].rearrange("p (t h d) -> p t h d", t=TT, d=HD),
                                  b.to_broadcast([P, TT, 4 * AG, HD]), ALU.add).then_inc(v_done.sem, 1)

            def att_(g):
                def piece(r, rows):
                    dve.wait_ge(o_ps.sem, o_ps.of(r, g + 1))
                    o = ps_st[:, 1, :].rearrange("p (t h r) -> p t h r", t=TT, h=4)
                    dve.reciprocal(rden[:, :, :], o[:, :, :, HD]).then_inc(rden_done.sem, 1)
                    dve.wait_ge(rden_done.sem, rden_done.of(r, g + 1))
                    dve.tensor_tensor(att[:, :, 32 * g:32 * g + 32].rearrange("p t (h d) -> p t h d", h=4),
                                      o[:, :, :, 0:HD], rden[:, :, :].unsqueeze(3).to_broadcast([P, TT, 4, HD]),
                                      ALU.mult).then_inc(att_done.sem, 1)
                return piece

            def gate(j):
                def piece(r, rows):
                    dve.wait_ge(tanh_done.sem, tanh_done.of(r, j + 1))
                    dve.scalar_tensor_tensor(out=g_tanh[:, :], in0=g_tanh[:, :], scalar=1.0, in1=ps_c[:, :],
                                             op0=ALU.add, op1=ALU.mult).then_inc(g_lin_done.sem, 1)
                return piece

            def up(j):
                def piece(r, rows):
                    dve.wait_ge(up_ps.sem, up_ps.of(r, j + 1))
                    dve.scalar_tensor_tensor(out=ffh[:, j, :], in0=g_tanh[:, :], scalar=0.5, in1=ps_c[:, :],
                                             op0=ALU.mult, op1=ALU.mult).then_inc(ffh_done.sem, 1)
                return piece

            def res_(r, rows):
                dve.wait_ge(res_ps.sem, res_ps.of(r, 1))
                if has_past(r):
                    dve.wait_ge(res_held_done.sem, res_held_done.of(r - 1, 1))
                dve.tensor_copy(flat(res), ps_c[:, :]).then_inc(res_done.sem, 1)

            def store(r, rows):
                dve.wait_ge(y_ps.sem, y_ps.of(r, 1))
                dve.wait_ge(res_held_done.sem, res_held_done.of(r, 1))
                if has_past(r):
                    dve.wait_ge(stored.sem, stored.of(r - 1, 16))
                dve.tensor_tensor(flat(y), ps_c[:, :], flat(res_held), ALU.add).then_inc(y_done.sem, 1)

            def attention(slot, rows):
                n = (slot + S_AHEAD) % SLOTS
                who = "a" if slot + S_AHEAD < SLOTS else "c"
                if who in rows:
                    g, qt, h = n // 16, n // 4 % TT, n % 4
                    dve.wait_ge(s_ps.sem, s_ps.of(rows[who], n + 1))
                    dve.tensor_reduce(mx[:, g, qt, h:h + 1], ps_s[:, n % 2, :], AX.X, ALU.max).then_inc(s_max.sem, 1)

            pieces = {"ln1": norm_stats(xin, x_loaded, 16, ln1, ln1_stats, ln1_var, ln1_veps),
                      "xn": normalise(xn, xin, ln1, ln1_rstd, xn_done),
                      "dx": dx_, "z": z_,
                      "lnz": norm_stats(z, z_done, 1, lnz, lnz_stats, lnz_var, lnz_veps), "u": u_,
                      "ffn2": ffn2, "x1_3": x1_,
                      "ln2": norm_stats(x1, x1_done, 1, ln2, ln2_stats, ln2_var, ln2_veps),
                      "xm": normalise(xm, x1, ln2, ln2_rstd, xm_done),
                      "query": low(0, q_hi, q_lo, "q"), "key": low(1, k_hi, k_lo, "k"), "values": values, "res": res_, "store": store}
            for h in range(NH):
                pieces[f"rec{2 * h + 1}"] = scan(h)
                pieces[f"head{h}"] = head(h)
            for t in range(TT):
                pieces[f"sum{t}"] = sum_(t)
            for half in range(2):
                pieces[f"norm{half}"] = norm(half)
            for j in range(GC):
                pieces[f"gate{j}"] = gate(j)
                pieces[f"up{j}"] = up(j)
            for g in range(AG):
                pieces[f"max{g}"] = split_max(g)
                pieces[f"att{g}"] = att_(g)
            pipeline(dve, attention, pieces)

        @block.gpsimd
        def _(pool):
            pool.memset(ident[:, :], 0.0).then_inc(pool_const.sem, 1)
            pool.memset(zeros[:, :], 0.0).then_inc(pool_const.sem, 1)
            pool.memset(ones_row, 1.0).then_inc(pool_const.sem, 1)
            pool.memset(k_st[:, :, :].bitcast(F32), 0.0).then_inc(pool_const.sem, 1)
            pool.memset(q_st[:, :, :].bitcast(F32), 0.0).then_inc(pool_const.sem, 1)
            pool.memset(neg_half[:, :], -0.5).then_inc(pool_const.sem, 1)
            pool.memset(vv[:, :, :, :], 0.0).then_inc(pool_const.sem, 1)
            pool.wait_ge(pool_const.sem, POOL_CONST - 2)
            pool.affine_select(out=ident[:, :], in_=ident[:, :], compare_op=ALU.not_equal, fill=1.0, base=0,
                               pattern=[[-1, P]], channel_multiplier=1).then_inc(pool_const.sem, 1)
            pool.memset(vv[:, :, :, HD:HD + 1], 1.0).then_inc(pool_const.sem, 1)
            pool.wait_ge(const_ready.sem, 1)

            def rstd(buf, veps, done):
                def piece(r, rows):
                    pool.wait_ge(veps.sem, veps.of(r, 1))
                    pool.tensor_tensor(buf[:, :, 9], buf[:, :, 8], neg_half[:, 0:TT], ALU.pow).then_inc(done.sem, 1)
                return piece

            def x_bias_(r, rows):
                pool.wait_ge(xn_done.sem, xn_done.of(r, TT))
                if has_past(r):
                    pool.wait_ge(x1_done.sem, x1_done.of(r - 1, 1))
                pool.tensor_tensor(x_bias[:, :, :], xin[:, :, :], pb2[:, :].unsqueeze(1).to_broadcast([P, TT, P]),
                                   ALU.add).then_inc(x_bias_done.sem, 1)

            def dx_(r, rows):
                pool.wait_ge(const_ready.sem, 1)
                pool.wait_ge(dx_done.sem, dx_done.of(r, 1))
                pool.tensor_scalar(flat(dx_b), flat(dx), 1.0 / NH, 0.0, ALU.mult, ALU.add).then_inc(dx_b_done.sem, 1)
                pool.wait_ge(dx_b_done.sem, dx_b_done.of(r, 1))
                pool.tensor_tensor(dx_b[:, :, :], dx_b[:, :, :], hw_b[:, :].unsqueeze(1).to_broadcast([P, TT, P]),
                                   ALU.add).then_inc(dx_b_done.sem, 1)

            def norm(half):
                c = slice(half * TT * NH // 2, (half + 1) * TT * NH // 2)

                def piece(r, rows):
                    pool.wait_ge(head_var.sem, head_var.of(r, 7 * half + 7))
                    pool.tensor_tensor(hv[:, 6, c], hv[:, 5, c], neg_half[:, c], ALU.pow).then_inc(head_rstd.sem, 1)
                    pool.wait_ge(head_rstd.sem, head_rstd.of(r, half + 1))
                    pool.tensor_tensor(hv[:, 0, c], hv[:, 7, c], hv[:, 6, c], ALU.mult).then_inc(head_shift.sem, 1)
                    pool.wait_ge(const_ready.sem, 1)
                    pool.wait_ge(head_shift.sem, head_shift.of(r, half + 1))
                    for t in range(half * TT // 2, (half + 1) * TT // 2):
                        for h in range(NH):
                            k = t * NH + h
                            ins = pool.tensor_scalar(prod[:, t, h, :], prod[:, t, h, :], hv[:, 6, k:k + 1],
                                                     hv[:, 0, k:k + 1], ALU.mult, ALU.add)
                        ins.then_inc(head_norm.sem, 1)
                        pool.wait_ge(head_norm.sem, head_norm.of(r, t + 1))
                        pool.tensor_tensor(prod[:, t, :, :].rearrange("p h k -> p (h k)"),
                                           prod[:, t, :, :].rearrange("p h k -> p (h k)"), hw_g[:, :],
                                           ALU.mult).then_inc(head_scaled.sem, 1)
                return piece

            def z_(r, rows):
                pool.wait_ge(z_done.sem, z_done.of(r, 1))
                pool.tensor_tensor(z_b[:, :, :], z[:, :, :], along("nb"), ALU.add).then_inc(z_b_done.sem, 1)

            def x1_(r, rows):
                if has_past(r):
                    pool.wait_ge(res_held_done.sem, res_held_done.of(r - 1, 1))
                pool.wait_ge(x1_done.sem, x1_done.of(r, 1))
                pool.tensor_tensor(x1_b[:, :, :], x1[:, :, :], along("ap"), ALU.add).then_inc(x1_b_done.sem, 1)

            def hold(r, rows):
                pool.wait_ge(res_done.sem, res_done.of(r, 1))
                if has_past(r):
                    pool.wait_ge(y_done.sem, y_done.of(r - 1, 1))
                pool.tensor_tensor(flat(res_held), flat(res), flat(x1_b), ALU.add).then_inc(res_held_done.sem, 1)

            pieces = {"ln1": rstd(ln1, ln1_veps, ln1_rstd), "lnz": rstd(lnz, lnz_veps, lnz_rstd),
                      "ln2": rstd(ln2, ln2_veps, ln2_rstd), "x_bias": x_bias_, "dx": dx_, "norm0": norm(0), "norm1": norm(1), "z": z_,
                      "x1_3": x1_, "hold": hold}
            pipeline(pool, lambda slot, rows: None, pieces)


def kernel(**inputs):
    import concourse.bacc as bacc
    from concourse.bass_utils import run_bass_kernel_spmd

    a = {k: np.asarray(v) for k, v in inputs.items()}

    def g0(name):
        return a["L0_attn_" + name]

    def heads(m):
        return m.transpose(2, 0, 1).reshape(P, NH * P)

    def chunks(m):
        return m.reshape(-1, P, m.shape[1]).transpose(1, 0, 2).reshape(P, -1)

    parts = {"wa": heads(g0("Wa_w")), "wb": heads(g0("Wb_w")), "c": heads(g0("C_w")), "d": g0("D_w").T,
             "wout": g0("Wout_w").T, "f1": g0("ffn1_w").T, "f2": chunks(g0("ffn2_w").T), "proj": g0("proj_w").T,
             "r1": a["L0_ffn_W1"], "r2": chunks(a["L0_ffn_W2"]), "qkv": a["L1_attn_w_qkv"], "ap": a["L1_attn_w_proj"]}
    w_pack = np.ascontiguousarray(np.concatenate([parts[n] for n in W_COLS], axis=1))
    wi_pack = np.ascontiguousarray(np.concatenate(
        [a["L1_ffn_w_gate"].T, a["L1_ffn_w_up"].T, chunks(a["L1_ffn_w_down"].T)], axis=1))
    bqkv = a["L1_attn_b_qkv"]
    cols = {"wa": g0("Wa_b").T, "wb": g0("Wb_b").T, "f1": g0("ffn1_b").reshape(FC, P).T, "f2": g0("ffn2_b")[:, None],
            "r1": a["L0_ffn_b1"].reshape(FC, P).T, "q": bqkv[0:P, None], "k": bqkv[P:2 * P, None]}
    b_pack = np.ascontiguousarray(np.concatenate([cols[n] for n in B_COLS], axis=1))
    rows = {"d": g0("D_b"), "wout": g0("Wout_b"), "ng": g0("norm_g"), "nb": g0("norm_b"), "proj": g0("proj_b"),
            "r2": a["L0_ffn_b2"], "v": bqkv[2 * P:], "ap": a["L1_attn_b_proj"], "hw": g0("head_w"),
            "hng": g0("hn_g").reshape(-1), "hnb": g0("hn_b").reshape(-1)}
    r_pack = np.ascontiguousarray(np.concatenate([rows[n] for n in R_COLS])[None, :])
    arrays = {"x": np.ascontiguousarray(g0("emb").reshape(ROWS * L, P)), "w_pack": w_pack, "wi_pack": wi_pack,
              "b_pack": b_pack, "r_pack": r_pack, "cb": np.ascontiguousarray(g0("C_b").reshape(1, NH * P))}

    nc = bacc.Bacc("TRN2", target_bir_lowering=False, num_devices=1)
    args = [nc.dram_tensor("in_" + n, v.shape, mybir.dt.from_np(v.dtype), kind="ExternalInput").ap()
            for n, v in arrays.items()]
    args.append(nc.dram_tensor("out", (ROWS * L, P), F32, kind="ExternalOutput").ap())
    two_block_model(nc, *args)
    r = run_bass_kernel_spmd(nc, [{"in_" + n: v for n, v in arrays.items()}], core_ids=[0])
    return r.results[0]["out"].reshape(ROWS, L, P)
```

```python
from contextlib import ExitStack

import numpy as np

import concourse.bass as bass
from concourse import mybir

F32 = mybir.dt.float32
F32R = mybir.dt.float32r
I32 = mybir.dt.int32
ALU = mybir.AluOpType
ACT = mybir.ActivationFunctionType
AX = mybir.AxisListType

P = 128
ROWS = 8
L = 512
TT = L // P
NH = 8
FC = 4
GC = 3
HD = 8
AG = 4
SLOTS = 4 * AG * TT
EPS = 1e-5
DX_AFTER = 5
BIAS_AT = slice(32, 34)
DEQUANT = float(np.float32(1.0 / 127.0))
SM_SCALE = HD ** -0.5
POOL_CONST = 10
WEIGH_SLOT = 1
ATT_SLOT = 4
S_AHEAD = 20

W_COLS = {}
_at = 0
for _name, _n in (("c", NH * P), ("wout", P), ("f1", FC * P), ("f2", FC * P), ("proj", P), ("r2", FC * P), ("ap", P)):
    W_COLS[_name] = _at
    _at += _n
W_TOTAL = _at
WS_COLS = {}
_at = 0
for _name, _n in (("wa", NH * P), ("wb", NH * P), ("d", P), ("r1", FC * P), ("qkv", 3 * P)):
    WS_COLS[_name] = _at
    _at += _n
WS_LOADED = _at
WS_COLS["gate"], WS_COLS["up"] = _at, _at + GC * P
WS_TOTAL = _at + 2 * GC * P
B_COLS = {}
_at = 0
for _name, _n in (("wa", NH), ("wb", NH), ("f1", FC), ("f2", 1), ("r1", FC), ("q", 1), ("k", 1)):
    B_COLS[_name] = _at
    _at += _n
B_TOTAL = _at
R_COLS = {}
_at = 0
for _name, _n in (("d", P), ("wout", P), ("ng", P), ("nb", P), ("proj", P), ("r2", P), ("v", P), ("ap", P),
                  ("hw", NH), ("hng", NH * P), ("hnb", NH * P)):
    R_COLS[_name] = _at
    _at += _n
R_TOTAL = _at
R_KEEP = R_COLS["hw"]


class Signal:

    def __init__(self, sem, per_row):
        self.sem, self.per_row = sem, per_row

    def of(self, row, n):
        return row * self.per_row + n


def two_block_model(nc, x, w_pack, ws_pack, wi_pack, b_pack, r_pack, cb, out):
    with ExitStack() as ctx:
        def sb(name, shape, dt=F32):
            return ctx.enter_context(nc.sbuf_tensor(name, shape, dt))

        def sig(name, per_row=1):
            return Signal(ctx.enter_context(nc.semaphore(name)), per_row)

        w = sb("w", [P, W_TOTAL])
        bias = sb("bias", [P, B_TOTAL])
        rowv = sb("rowv", [P, R_KEEP])
        ws_hi = sb("ws_hi", [P, WS_TOTAL], F32R)
        ws_lo = sb("ws_lo", [P, WS_TOTAL], F32R)
        w_down = sb("w_down", [P, GC * P])
        hw_g = sb("hw_g", [P, NH * P])
        hw_b = sb("hw_b", [P, P])
        pb2 = rowv[:, R_COLS["proj"]:R_COLS["proj"] + P]
        ident = sb("ident", [P, P])
        small = sb("small", [P, NH * P], F32R)
        cb_split = small[BIAS_AT, :]
        m_neg = small[0:8, 0:L]
        zeros = small[64:96, 0:L].bitcast(F32)
        cb_mask = sb("cb_mask", [P, 1])
        ones2 = sb("ones2", [P, P], F32R)[BIAS_AT, :]
        neg_half = sb("neg_half", [P, TT * NH])
        per_head = sb("per_head", [P, 1])

        xin = sb("xin", [P, TT, P])
        x_bias = sb("x_bias", [P, TT, P])
        xn = sb("xn", [P, TT, P])
        ln1 = sb("ln1", [P, TT, 12])
        xnT_hi = sb("xnT_hi", [P, L], F32R)
        xnT_lo = sb("xnT_lo", [P, L], F32R)
        decay = sb("decay", [P, 2, L])
        drive = sb("drive", [P, 2, L])
        hs = sb("hs", [P, NH, L])
        dx = sb("dx", [P, TT, P])
        dx_b = sb("dx_b", [P, TT, P])
        relu = sb("relu", [P, FC, L])
        prod = sb("prod", [P, TT, NH, P])
        hst = sb("hst", [P, TT * NH, 6])
        hv = sb("hv", [P, 8, TT * NH])
        hsum = sb("hsum", [P, TT, P])
        z = sb("z", [P, TT, P])
        zn = sb("zn", [P, TT, P])
        xm = zn
        lnz = sb("lnz", [P, TT, 12])
        z_b = sb("z_b", [P, TT, P])
        uT = sb("uT", [P, L])
        shT = uT
        gel = sb("gel", [P, FC, L])
        hT = uT
        x1 = sb("x1", [P, TT, P])

        x1_b = sb("x1_b", [P, TT, P])
        ln2 = sb("ln2", [P, TT, 12])
        xmT_hi = sb("xmT_hi", [P, L], F32R)
        xmT_lo = sb("xmT_lo", [P, L], F32R)
        q_hi = sb("q_hi", [P, L], F32R)
        q_lo = sb("q_lo", [P, L], F32R)
        k_hi = sb("k_hi", [P, L], F32R)
        k_lo = sb("k_lo", [P, L], F32R)
        q_st = sb("q_st", [P, AG, L], F32R)
        k_st = sb("k_st", [P, AG, L], F32R)
        mx = sb("mx", [P, AG, TT, 4])
        mx_split = sb("mx_split", [P, TT, 2, 4], F32R)
        vv = sb("vv", [P, TT, AG * 4, 32])
        prob = sb("prob", [P, 2, 4, L])
        oT = sb("oT", [P, L])
        rden = sb("rden", [P, TT, 4])
        att = sb("att", [P, TT, P])
        attT = sb("attT", [P, TT * P])
        g_tanh = sb("g_tanh", [P, L])
        ffh = gel
        res = sb("res", [P, TT, P])
        res_held = sb("res_held", [P, TT, P])
        y = res_held

        r_tmp = prod[:, 0:3, :, :].rearrange("p t h k -> p (t h k)")
        cb_raw = prod[BIAS_AT, 3, :, :].rearrange("p h k -> p (h k)")
        cb_hi = relu[BIAS_AT, 0:2, :].rearrange("p h n -> p (h n)")
        ones_row = relu[64:68, :, :]
        whole = gel[:, 0:2, :].rearrange("p j n -> p (j n)")[:, 0:2 * GC * P]
        ws_tmp = hs[:, :, :].rearrange("p h n -> p (h n)")
        wi = prob[:, :, :, :].rearrange("p a b n -> p (a b n)").bitcast(I32)

        ps0 = ctx.enter_context(nc.psum_tensor("ps0", [P, 2, L], F32))
        ps_s = ctx.enter_context(nc.psum_tensor("ps_s", [P, 2, L], F32))
        ps_st = ctx.enter_context(nc.psum_tensor("ps_st", [P, 2, L], F32))
        ps_pv = ctx.enter_context(nc.psum_tensor("ps_pv", [P, L], F32))
        ps_c = ctx.enter_context(nc.psum_tensor("ps_c", [P, L], F32))

        w_loaded, ws_loaded, wi_loaded, b_loaded, r_loaded, cb_loaded = (
            sig(n) for n in ("w_loaded", "ws_loaded", "wi_loaded", "b_loaded", "r_loaded", "cb_loaded"))
        pool_const, k_ones, su, ws_ready, heads_ready, const_ready = (
            sig(n) for n in ("pool_const", "k_ones", "su", "ws_ready", "heads_ready", "const_ready"))

        x_loaded = sig("x_loaded", 16)
        ln1_stats, ln1_var, ln1_veps, ln1_rstd = sig("ln1_stats", 4), sig("ln1_var", 4), sig("ln1_veps", 2), sig("ln1_rstd", 2)
        xn_done, xnT_ps, xnT_kept, xnT_done = sig("xn_done"), sig("xnT_ps"), sig("xnT_kept"), sig("xnT_done")
        x_bias_done = sig("x_bias_done")
        rec_ps, decay_done, drive_done, scan_done = sig("rec_ps", 2 * NH), sig("decay_done", NH), sig("drive_done", NH), sig("scan_done", NH)
        dx_ps, dx_done, dx_b_done = sig("dx_ps"), sig("dx_done"), sig("dx_b_done", 2)
        relu_ps, relu_done = sig("relu_ps", FC), sig("relu_done", FC)
        head_ps, prod_done, head_stats, head_var, head_rstd = sig("head_ps", 2 * TT), sig("prod_done", 2 * TT), sig("head_stats", 2 * TT), sig("head_var", 7 * TT), sig("head_rstd", TT)
        head_shift = sig("head_shift", TT)
        head_norm, head_norm_act, head_scaled, head_added, sum_done = sig("head_norm", TT), sig("head_norm_act", TT), sig("head_scaled", TT), sig("head_added", TT), sig("sum_done", 2 * TT)
        shT_ps, shT_done, z_ps, z_done, z_b_done = sig("shT_ps"), sig("shT_done"), sig("z_ps"), sig("z_done"), sig("z_b_done")
        lnz_stats, lnz_var, lnz_veps, lnz_rstd = sig("lnz_stats", 4), sig("lnz_var", 4), sig("lnz_veps", 2), sig("lnz_rstd", 2)
        zn_done, zg_done, u_done, uT_ps, uT_done = sig("zn_done"), sig("zg_done"), sig("u_done"), sig("uT_ps"), sig("uT_done")
        f1_ps, f1_kept, gelu_done, f2_ps, hT_done, x1_ps, x1_done = sig("f1_ps", FC), sig("f1_kept", FC), sig("gelu_done"), sig("f2_ps"), sig("hT_done"), sig("x1_ps", TT), sig("x1_done")
        ln2_stats, ln2_var, ln2_veps, ln2_rstd = sig("ln2_stats", 4), sig("ln2_var", 4), sig("ln2_veps", 2), sig("ln2_rstd", 2)
        xm_done, xmT_ps, xmT_kept, xmT_done = sig("xm_done"), sig("xmT_ps"), sig("xmT_kept"), sig("xmT_done")
        x1_b_done = sig("x1_b_done")
        qk_ps, qk_hi, qk_lo = sig("qk_ps", 2), sig("qk_hi", 2), sig("qk_lo", 2)
        stacked = [sig(f"stacked{g}", 16 * 7) for g in range(AG)]
        s_ps, s_max = sig("s_ps", SLOTS), sig("s_max", SLOTS)
        mx_high, mx_low, m_ps, m_done = sig("mx_high", AG), sig("mx_low", AG), sig("m_ps", AG), sig("m_done", AG)
        m_placed = [sig(f"m_placed{g}", 32) for g in range(AG)]
        v_ps, v_done = sig("v_ps"), sig("v_done")
        st_ps, exp_done, pv_done = sig("st_ps", SLOTS), sig("exp_done", SLOTS), sig("pv_done", AG * TT)
        oT_done, o_ps, rden_done, att_done = sig("oT_done", AG), sig("o_ps", AG), sig("rden_done", AG), sig("att_done", AG)
        gate_ps, tanh_done, g_lin_done, up_ps, ffh_done = sig("gate_ps", GC), sig("tanh_done", GC), sig("g_lin_done", GC), sig("up_ps", GC), sig("ffh_done", GC)
        res_ps, res_done, res_held_done = sig("res_ps"), sig("res_done"), sig("res_held_done")
        attT_ps, attT_done, y_ps, y_done, stored = sig("attT_ps"), sig("attT_done"), sig("y_ps"), sig("y_done"), sig("stored", 16)

        def has_past(row):
            return not (isinstance(row, int) and row < 1)

        def wcol(name, i=0, n=P):
            return w[:, W_COLS[name] + i * P:W_COLS[name] + i * P + n]

        def ws(part, name, i):
            return part[:, WS_COLS[name] + i * P:WS_COLS[name] + (i + 1) * P]

        def bcol(name, i=0):
            return bias[:, B_COLS[name] + i:B_COLS[name] + i + 1]

        def along(name):
            return rowv[:, R_COLS[name]:R_COLS[name] + P].unsqueeze(1).to_broadcast([P, TT, P])

        def flat(t):
            return t[:, :, :].rearrange("p t n -> p (t n)")

        beside = {
            0: "stack3 a, rec7 n, uT c", 2: "values a", 3: "rec8 n", 4: "att3 t, ffn1_0 c", 6: "ffn1_1 c",
            7: "attT t, rec9 n", 8: "ffn1_2 c", 10: "ffn1_3 c, gelu c", 11: "dx n",
            12: "max1 a, store t, rec10 n, rec11 n", 13: "rec12 n", 14: "rec13 n", 15: "ffn2_0 c",
            16: "ffn2_1 c, rec14 n", 18: "rec15 n, ffn2_2 c", 19: "ffn2_3 c", 20: "att0 a, head0 n",
            21: "hold a, head1 n", 22: "x1_0 c, moments0 n", 23: "x1_1 c, moments1 n",
            24: "x1_2 c, x1_3 c, ln2a c", 27: "ln2 c, head2 n", 28: "max2 a, x_bias n, moments2 n",
            30: "norm0 n, head3 n, load f", 31: "moments3 n", 32: "xmT c, ln1a f", 33: "scale0 n",
            34: "query c, norm1 n, ln1 f", 35: "head4 n", 36: "att1 a, key c",
            37: "stack0 c, stack1 c, moments4 n, scale1 n", 38: "head5 n, gate0 c", 39: "moments5 n",
            40: "up0 c, norm2 n", 41: "head6 n", 42: "sum0 n, gate1 c", 43: "moments6 n, head7 n, sum1 n",
            44: "max3 a, relu0 n", 45: "moments7 n, scale2 n", 46: "up1 c, norm3 n, relu1 n",
            47: "relu2 n, sum2 n", 48: "gate2 c, stack2 c", 49: "sum3 n", 50: "up2 c, relu3 n, sum4 n",
            51: "sum5 n", 52: "att2 a, scale3 n", 53: "xnT f", 56: "sum6 n, rec0 f, rec1 f, sum7 n",
            57: "shT n, rec2 f", 58: "z n", 59: "lnza n", 60: "rec3 f, rec4 f, max0 c, lnz n",
            61: "res_0 c, rec5 f, u n, res_1 c", 63: "res_2 c, u2 n, rec6 f, res_3 c",
        }
        offset = {"t": -2, "a": -1, "c": 0, "n": 1, "f": 2}

        def step(i, lo, hi, attention, pieces, late):
            rows = {who: i + off for who, off in offset.items() if 0 <= lo + off and hi + off < ROWS}
            for slot in range(SLOTS + 1):
                if slot < SLOTS:
                    attention(slot, rows)
                for at in (slot - 1, slot):
                    for item in beside.get(at, "").split(", "):
                        name, _, who = item.partition(" ")
                        if who in rows and name in pieces and (name in late) == (at < slot):
                            pieces[name](rows[who], rows)

        def pipeline(eng, attention, pieces, late=()):
            first, last = 2, ROWS - 3
            for i in range(-2, first):
                step(i, i, i, attention, pieces, late)
            with eng.Fori(first, last + 1) as i:
                step(i, first, last, attention, pieces, late)
            for i in range(last + 1, ROWS + 2):
                step(i, i, i, attention, pieces, late)

        block = ctx.enter_context(nc.Block())

        @block.sync
        def _(sp):
            x_rows = x.rearrange("(b t p) e -> b p t e", b=ROWS, t=TT)
            out_rows = out.rearrange("(b t p) e -> b p t e", b=ROWS, t=TT)
            sp.dma_start(xin[:, :, :], x_rows[0]).then_inc(x_loaded.sem, 16)
            sp.dma_start(ws_tmp[:, 0:WS_LOADED], ws_pack).then_inc(ws_loaded.sem, 16)
            sp.dma_start(bias[:, :], b_pack).then_inc(b_loaded.sem, 16)
            sp.dma_start(rowv[:, :], r_pack[:, 0:R_KEEP].to_broadcast([P, R_KEEP])).then_inc(r_loaded.sem, 16)
            sp.dma_start(r_tmp[:, 0:R_TOTAL - R_KEEP],
                         r_pack[:, R_KEEP:].to_broadcast([P, R_TOTAL - R_KEEP])).then_inc(r_loaded.sem, 16)
            sp.dma_start(wi[:, 0:3 * GC * P], wi_pack).then_inc(wi_loaded.sem, 16)
            sp.dma_start(cb_raw, cb.to_broadcast([2, NH * P])).then_inc(cb_loaded.sem, 16)
            sp.dma_start(w[:, :], w_pack).then_inc(w_loaded.sem, 16)
            sp.wait_ge(pool_const.sem, POOL_CONST)
            for d in range(2):
                sp.dma_start(k_st[4 * d + 3:4 * d + 3 + 97:32, :, :].bitcast(F32),
                             ones_row).then_inc(k_ones.sem, 16)


            def load(r, rows):
                if isinstance(r, int) and r == 0:
                    return
                if has_past(r):
                    sp.wait_ge(x_bias_done.sem, x_bias_done.of(r - 1, 1))
                sp.dma_start(xin[:, :, :], x_rows[r]).then_inc(x_loaded.sem, 16)

            def stack(g):
                def piece(r, rows):
                    if g == 0:
                        sp.wait_ge(qk_lo.sem, qk_lo.of(r, 2))
                    if has_past(r):
                        sp.wait_ge(st_ps.sem, st_ps.of(r - 1, 16 * (g + 1)))
                    half = slice(32 * g, 32 * g + 32)
                    for j, (kp, qp) in enumerate(((k_hi, q_hi), (k_hi, q_lo), (k_lo, q_hi))):
                        for st, part in ((k_st, kp), (q_st, qp)):
                            sp.dma_start(st[j:j + 125:4, g, :].bitcast(F32),
                                         part[half, :].bitcast(F32)).then_inc(stacked[g].sem, 16)
                    sp.dma_start(q_st[3:3 + 125:4, g, :].bitcast(F32), zeros).then_inc(stacked[g].sem, 16)
                return piece

            def place_max(g):
                def piece(r, rows):
                    sp.wait_ge(m_done.sem, m_done.of(r, g + 1))
                    for d in range(2):
                        sp.dma_start(q_st[4 * d + 3:4 * d + 3 + 97:32, g, :].bitcast(F32),
                                     m_neg[4 * d:4 * d + 4, :].bitcast(F32)).then_inc(m_placed[g].sem, 16)
                return piece

            def store(r, rows):
                sp.wait_ge(y_done.sem, y_done.of(r, 1))
                sp.dma_start(out_rows[r], y[:, :, :]).then_inc(stored.sem, 16)

            pieces = {"load": load, "store": store}
            for g in range(AG):
                pieces[f"stack{g}"] = stack(g)
                pieces[f"max{g}"] = place_max(g)
            pipeline(sp, lambda slot, rows: None, pieces)
            sp.wait_ge(stored.sem, 16 * ROWS)

        @block.tensor
        def _(pe):
            pe.wait_ge(ws_ready.sem, 2)
            pe.wait_ge(pool_const.sem, POOL_CONST)


            def transposes(bank, src, signal):
                for t in range(TT):
                    mm = pe.transpose(bank[:, t * P:(t + 1) * P], src[:, t, :], ident[:, :])
                mm.then_inc(signal.sem, 1)

            def times_weights(bank, name, i, hi, lo):
                pe.matmul(bank, ws(ws_hi, name, i), hi[:, :], start=True, stop=False)
                pe.matmul(bank, ws(ws_lo, name, i), hi[:, :], start=False, stop=False)
                return pe.matmul(bank, ws(ws_hi, name, i), lo[:, :], start=False, stop=True)

            def row_times(bank, name, i, hi, lo):
                for t in range(TT):
                    cols = slice(t * P, (t + 1) * P)
                    pe.matmul(bank[:, cols], hi[:, cols], ws(ws_hi, name, i), start=True, stop=False)
                    pe.matmul(bank[:, cols], hi[:, cols], ws(ws_lo, name, i), start=False, stop=False)
                    mm = pe.matmul(bank[:, cols], lo[:, cols], ws(ws_hi, name, i), start=False, stop=True)
                return mm

            def xnT_(r, rows):
                pe.wait_ge(xn_done.sem, xn_done.of(r, 1))
                if has_past(r):
                    pe.wait_ge(relu_done.sem, relu_done.of(r - 1, FC - 1))
                transposes(ps0[:, 0, :], xn, xnT_ps)

            def rec(k):
                h = k // 2

                def decay_(r, rows):
                    pe.wait_ge(xnT_done.sem, xnT_done.of(r, 1))
                    if h == DX_AFTER:
                        pe.wait_ge(dx_done.sem, dx_done.of(r, 1))
                    elif h:
                        pe.wait_ge(decay_done.sem, decay_done.of(r, h))
                    elif has_past(r):
                        pe.wait_ge(relu_done.sem, relu_done.of(r - 1, FC))
                    times_weights(ps0[:, 1, :], "wa", h, xnT_hi, xnT_lo).then_inc(rec_ps.sem, 1)

                def drive_(r, rows):
                    if h:
                        pe.wait_ge(drive_done.sem, drive_done.of(r, h))
                    times_weights(ps0[:, 0, :], "wb", h, xnT_hi, xnT_lo).then_inc(rec_ps.sem, 1)
                return drive_ if k % 2 else decay_

            def dx_(r, rows):
                pe.wait_ge(decay_done.sem, decay_done.of(r, DX_AFTER))
                row_times(ps0[:, 1, :], "d", 0, xnT_hi, xnT_lo).then_inc(dx_ps.sem, 1)

            def head(k):
                t, half = divmod(k, 2)

                def piece(r, rows):
                    if k == 0:
                        if isinstance(r, int) and r == 0:
                            pe.wait_ge(w_loaded.sem, 16)
                            pe.wait_ge(k_ones.sem, 32)
                            pe.wait_ge(heads_ready.sem, 1)
                            pe.wait_ge(const_ready.sem, 1)
                        pe.wait_ge(scan_done.sem, scan_done.of(r, NH))
                        pe.wait_ge(drive_done.sem, drive_done.of(r, NH))
                    elif k == 1:
                        pe.wait_ge(decay_done.sem, decay_done.of(r, NH))
                    else:
                        pe.wait_ge(prod_done.sem, prod_done.of(r, k - 1))
                    bank = ps0[:, half, :]
                    pe.matmul(bank, ones2, cb_split[:, half * L:(half + 1) * L], start=True, stop=False,
                              skip_group_check=True)
                    for h in range(4):
                        mm = pe.matmul(bank[:, h * P:(h + 1) * P], hs[:, 4 * half + h, t * P:(t + 1) * P],
                                       wcol("c", 4 * half + h), start=False, stop=(h == 3),
                                       skip_group_check=True)
                    mm.then_inc(head_ps.sem, 1)
                return piece

            def relu_(j):
                def piece(r, rows):
                    if j < 2:
                        pe.wait_ge(prod_done.sem, prod_done.of(r, 2 * TT - 1 + j))
                    else:
                        pe.wait_ge(relu_done.sem, relu_done.of(r, j - 1))
                    times_weights(ps0[:, j % 2, :], "r1", j, xnT_hi, xnT_lo).then_inc(relu_ps.sem, 1)
                return piece

            def shT_(r, rows):
                pe.wait_ge(sum_done.sem, sum_done.of(r, 2 * TT))
                if has_past(r):
                    pe.wait_ge(ffh_done.sem, ffh_done.of(r - 1, GC))
                transposes(ps_c[:, :], hsum, shT_ps)

            def values(r, rows):
                if "c" in rows:
                    pe.wait_ge(uT_done.sem, uT_done.of(rows["c"], 1))
                else:
                    pe.wait_ge(res_done.sem, res_done.of(r, 1))
                row_times(ps_c[:, :], "qkv", 2, xmT_hi, xmT_lo).then_inc(v_ps.sem, 1)

            def z_(r, rows):
                pe.wait_ge(shT_done.sem, shT_done.of(r, 1))
                for t in range(TT):
                    mm = pe.matmul(ps_c[:, t * P:(t + 1) * P], shT[:, t * P:(t + 1) * P], wcol("wout"),
                                   start=True, stop=True)
                mm.then_inc(z_ps.sem, 1)

            def attT_(r, rows):
                pe.wait_ge(att_done.sem, att_done.of(r, AG))
                if "c" in rows:
                    pe.wait_ge(f1_kept.sem, f1_kept.of(rows["c"], 2))
                elif "a" in rows:
                    pe.wait_ge(v_done.sem, v_done.of(rows["a"], 1))
                transposes(ps_c[:, :], att, attT_ps)

            def store(r, rows):
                pe.wait_ge(attT_done.sem, attT_done.of(r, 1))
                if "c" in rows:
                    pe.wait_ge(f1_kept.sem, f1_kept.of(rows["c"], FC))
                for t in range(TT):
                    mm = pe.matmul(ps_c[:, t * P:(t + 1) * P], attT[:, t * P:(t + 1) * P], wcol("ap"),
                                   start=True, stop=True)
                mm.then_inc(y_ps.sem, 1)

            def uT_(r, rows):
                pe.wait_ge(u_done.sem, u_done.of(r, 1))
                if has_past(r):
                    pe.wait_ge(res_done.sem, res_done.of(r - 1, 1))
                transposes(ps_c[:, :], zn, uT_ps)

            def ffn1(j):
                def piece(r, rows):
                    if j == 0:
                        pe.wait_ge(uT_done.sem, uT_done.of(r, 1))
                        if "a" in rows:
                            pe.wait_ge(v_done.sem, v_done.of(rows["a"], 1))
                    else:
                        pe.wait_ge(f1_kept.sem, f1_kept.of(r, j))
                        if j == 2 and "t" in rows:
                            pe.wait_ge(attT_done.sem, attT_done.of(rows["t"], 1))
                    pe.matmul(ps_c[:, :], wcol("f1", j), uT[:, :], start=True, stop=True).then_inc(f1_ps.sem, 1)
                return piece

            def ffn2(j):
                def piece(r, rows):
                    if j == 0:
                        pe.wait_ge(gelu_done.sem, gelu_done.of(r, 1))
                        if "t" in rows:
                            pe.wait_ge(y_done.sem, y_done.of(rows["t"], 1))
                    mm = pe.matmul(ps_c[:, :], wcol("f2", j), gel[:, j, :], start=(j == 0), stop=(j == FC - 1))
                    if j == FC - 1:
                        mm.then_inc(f2_ps.sem, 1)
                return piece

            def x1_(t):
                def piece(r, rows):
                    if t == 0:
                        pe.wait_ge(relu_done.sem, relu_done.of(r, FC))
                        pe.wait_ge(hT_done.sem, hT_done.of(r, 1))
                    cols = slice(t * P, (t + 1) * P)
                    for j in range(FC):
                        pe.matmul(ps_c[:, cols], relu[:, j, cols], wcol("r2", j), start=(j == 0), stop=False)
                    pe.matmul(ps_c[:, cols], hT[:, cols], wcol("proj"), start=False, stop=True).then_inc(x1_ps.sem, 1)
                return piece

            def xmT_(r, rows):
                pe.wait_ge(xm_done.sem, xm_done.of(r, 1))
                transposes(ps_c[:, :], xm, xmT_ps)

            def query(r, rows):
                pe.wait_ge(xmT_done.sem, xmT_done.of(r, 1))
                times_weights(ps_c[:, :], "qkv", 0, xmT_hi, xmT_lo).then_inc(qk_ps.sem, 1)

            def key(r, rows):
                pe.wait_ge(qk_lo.sem, qk_lo.of(r, 1))
                times_weights(ps_c[:, :], "qkv", 1, xmT_hi, xmT_lo).then_inc(qk_ps.sem, 1)

            def gate(j):
                def piece(r, rows):
                    if j == 0:
                        pe.wait_ge(qk_lo.sem, qk_lo.of(r, 2))
                    else:
                        pe.wait_ge(ffh_done.sem, ffh_done.of(r, j))
                    times_weights(ps_c[:, :], "gate", j, xmT_hi, xmT_lo).then_inc(gate_ps.sem, 1)
                return piece

            def up(j):
                def piece(r, rows):
                    pe.wait_ge(g_lin_done.sem, g_lin_done.of(r, j + 1))
                    times_weights(ps_c[:, :], "up", j, xmT_hi, xmT_lo).then_inc(up_ps.sem, 1)
                return piece

            def res_(t):
                def piece(r, rows):
                    if t == 0:
                        pe.wait_ge(ffh_done.sem, ffh_done.of(r, GC))
                        if "n" in rows:
                            pe.wait_ge(z_done.sem, z_done.of(rows["n"], 1))
                    for j in range(GC):
                        mm = pe.matmul(ps_c[:, t * P:(t + 1) * P], ffh[:, j, t * P:(t + 1) * P],
                                       w_down[:, j * P:(j + 1) * P], start=(j == 0), stop=(j == GC - 1))
                    if t == TT - 1:
                        mm.then_inc(res_ps.sem, 1)
                return piece

            def turn_max(g):
                def piece(r, rows):
                    pe.wait_ge(mx_low.sem, mx_low.of(r, g + 1))
                    for t in range(TT):
                        mm = pe.transpose(ps_s[0:8, 1, t * P:(t + 1) * P],
                                          mx_split[:, t, :, :].rearrange("p k h -> p (k h)").bitcast(F32),
                                          ident[:, :])
                    mm.then_inc(m_ps.sem, 1)
                return piece

            def turn_att(g):
                def piece(r, rows):
                    pe.wait_ge(oT_done.sem, oT_done.of(r, g + 1))
                    k = ATT_SLOT + 16 * (g + 1)
                    if g < AG - 1:
                        pe.wait_ge(exp_done.sem, exp_done.of(r, k))
                    elif "a" in rows:
                        pe.wait_ge(exp_done.sem, exp_done.of(r + 1, k - SLOTS))
                    for t in range(TT):
                        mm = pe.transpose(ps_st[:, 1, t * P:(t + 1) * P], oT[:, t * P:(t + 1) * P], ident[:, :])
                    mm.then_inc(o_ps.sem, 1)
                return piece

            def scores(r, n):
                g, qt, h = n // 16, n // 4 % TT, n % 4
                if n % 16 == 0:
                    pe.wait_ge(stacked[g].sem, stacked[g].of(r, 16 * 7))
                if n == 1 and has_past(r):
                    pe.wait_ge(m_done.sem, m_done.of(r - 1, AG))
                elif n % 16 == 1 and n > 1:
                    pe.wait_ge(m_done.sem, m_done.of(r, g))
                elif n >= 2:
                    pe.wait_ge(s_max.sem, s_max.of(r, n - 1))
                elif has_past(r):
                    pe.wait_ge(s_max.sem, s_max.of(r - 1, SLOTS - 1))
                part = slice(32 * h, 32 * h + 32)
                pe.matmul(ps_s[:, n % 2, :], q_st[part, g, qt * P:(qt + 1) * P], k_st[part, g, :],
                          start=True, stop=True).then_inc(s_ps.sem, 1)

            def scores_t(r, n, rows):
                g, kt, h = n // 16, n // 4 % TT, n % 4
                if n % 16 == 0:
                    pe.wait_ge(m_placed[g].sem, m_placed[g].of(r, 32))
                if n == ATT_SLOT + 1 and "t" in rows:
                    pe.wait_ge(att_done.sem, att_done.of(rows["t"], AG))
                elif n > 16 and n % 16 == ATT_SLOT + 1:
                    pe.wait_ge(att_done.sem, att_done.of(r, g))
                elif n >= 2:
                    pe.wait_ge(exp_done.sem, exp_done.of(r, n - 1))
                elif has_past(r):
                    pe.wait_ge(exp_done.sem, exp_done.of(r - 1, SLOTS - 1 + n))
                part = slice(32 * h, 32 * h + 32)
                pe.matmul(ps_st[:, n % 2, :], k_st[part, g, kt * P:(kt + 1) * P], q_st[part, g, :],
                          start=True, stop=True).then_inc(st_ps.sem, 1)

            def weigh(r, u):
                g, kt = divmod(u, TT)
                pe.wait_ge(exp_done.sem, exp_done.of(r, 4 * u + 4))
                if u == 0:
                    pe.wait_ge(v_done.sem, v_done.of(r, 1))
                if kt == 0:
                    if g:
                        pe.wait_ge(oT_done.sem, oT_done.of(r, g))
                    elif has_past(r):
                        pe.wait_ge(oT_done.sem, oT_done.of(r - 1, AG))
                for h in range(4):
                    mm = pe.matmul(ps_pv[32 * h:32 * h + 32, :], vv[:, kt, 4 * g + h, :], prob[:, u % 2, h, :],
                                   start=(kt == 0), stop=(kt == TT - 1))
                mm.then_inc(pv_done.sem, 1)

            def attention(slot, rows):
                if slot == WEIGH_SLOT and "t" in rows:
                    weigh(rows["t"], SLOTS // 4 - 1)
                if slot > 4 and slot % 4 == WEIGH_SLOT and "a" in rows:
                    weigh(rows["a"], slot // 4 - 1)
                if "a" in rows:
                    scores_t(rows["a"], slot, rows)
                n = slot + S_AHEAD
                if n < SLOTS and "a" in rows:
                    scores(rows["a"], n)
                if n >= SLOTS and "c" in rows:
                    scores(rows["c"], n - SLOTS)

            pieces = {"xnT": xnT_, "dx": dx_, "shT": shT_, "z": z_, "uT": uT_, "xmT": xmT_,
                      "query": query, "key": key, "values": values, "attT": attT_, "store": store}
            for k in range(2 * NH):
                pieces[f"rec{k}"] = rec(k)
                pieces[f"head{k // 2}"] = head(k // 2)
            for k in range(4):
                pieces[f"relu{k}"] = relu_(k)
                pieces[f"ffn1_{k}"] = ffn1(k)
                pieces[f"ffn2_{k}"] = ffn2(k)
                pieces[f"x1_{k}"] = x1_(k)
                pieces[f"res_{k}"] = res_(k)
                pieces[f"max{k}"] = turn_max(k)
                pieces[f"att{k}"] = turn_att(k)
            for j in range(GC):
                pieces[f"gate{j}"] = gate(j)
                pieces[f"up{j}"] = up(j)
            pipeline(pe, attention, pieces)


        @block.scalar
        def _(act):
            act.wait_ge(b_loaded.sem, 16)

            def copy_out(dst, src, ps, done):
                def piece(r, rows):
                    act.wait_ge(ps.sem, ps.of(r, 1))
                    act.activation(dst, src, ACT.Copy).then_inc(done.sem, 1)
                return piece

            def rec(k):
                h = k // 2

                def decay_(r, rows):
                    act.wait_ge(rec_ps.sem, rec_ps.of(r, k + 1))
                    if h >= 2:
                        act.wait_ge(scan_done.sem, scan_done.of(r, h - 1))
                    act.activation(decay[:, h % 2, :], ps0[:, 1, :], ACT.Tanh, bias=bcol("wa", h))\
                        .then_inc(decay_done.sem, 1)

                def drive_(r, rows):
                    act.wait_ge(rec_ps.sem, rec_ps.of(r, k + 1))
                    act.activation(drive[:, h % 2, :], ps0[:, 0, :], ACT.Identity, bias=bcol("wb", h))\
                        .then_inc(drive_done.sem, 1)
                return drive_ if k % 2 else decay_

            def relu_(j):
                def piece(r, rows):
                    act.wait_ge(relu_ps.sem, relu_ps.of(r, j + 1))
                    act.activation(relu[:, j, :], ps0[:, j % 2, :], ACT.Relu, bias=bcol("r1", j))\
                        .then_inc(relu_done.sem, 1)
                return piece

            def ffn1(j):
                def piece(r, rows):
                    act.wait_ge(f1_ps.sem, f1_ps.of(r, j + 1))
                    act.activation(gel[:, j, :], ps_c[:, :], ACT.Identity, bias=bcol("f1", j)).then_inc(f1_kept.sem, 1)
                return piece

            def gelu(r, rows):
                act.wait_ge(f1_kept.sem, f1_kept.of(r, FC))
                act.activation(flat(gel), flat(gel), ACT.Gelu).then_inc(gelu_done.sem, 1)

            def scale(t):
                def piece(r, rows):
                    act.wait_ge(head_shift.sem, head_shift.of(r, t + 1))
                    for h in range(NH // 2, NH):
                        k = t * NH + h
                        ins = act.activation(prod[:, t, h, :], prod[:, t, h, :], ACT.Identity,
                                             scale=hv[:, 6, k:k + 1], bias=hv[:, 0, k:k + 1])
                    ins.then_inc(head_norm_act.sem, 1)
                return piece

            def res_(r, rows):
                act.wait_ge(res_ps.sem, res_ps.of(r, 1))
                if has_past(r):
                    act.wait_ge(res_held_done.sem, res_held_done.of(r - 1, 1))
                act.activation(flat(res), ps_c[:, :], ACT.Copy).then_inc(res_done.sem, 1)

            def high(part, hi, name):
                def piece(r, rows):
                    act.wait_ge(qk_ps.sem, qk_ps.of(r, part + 1))
                    act.activation(hi[:, :], ps_c[:, :], ACT.Identity, bias=bcol(name)).then_inc(qk_hi.sem, 1)
                return piece

            def split_max(g):
                def piece(r, rows):
                    act.wait_ge(m_ps.sem, m_ps.of(r, g + 1))
                    act.activation(m_neg, ps_s[0:8, 1, :], ACT.Copy, scale=-1.0).then_inc(m_done.sem, 1)
                return piece

            def gate(j):
                def piece(r, rows):
                    act.wait_ge(gate_ps.sem, gate_ps.of(r, j + 1))
                    act.activation(g_tanh[:, :], ps_c[:, :], ACT.Tanh, scale=0.5).then_inc(tanh_done.sem, 1)
                return piece

            def keep_weighed(r, g):
                act.wait_ge(pv_done.sem, pv_done.of(r, TT * (g + 1)))
                act.activation(oT[:, :], ps_pv[:, :], ACT.Copy).then_inc(oT_done.sem, 1)

            def attention(slot, rows):
                if "a" in rows:
                    r, buf, h = rows["a"], slot // 4 % 2, slot % 4
                    act.wait_ge(st_ps.sem, st_ps.of(r, slot + 1))
                    act.activation(prob[:, buf, h, :], ps_st[:, slot % 2, :], ACT.Exp, scale=SM_SCALE)\
                        .then_inc(exp_done.sem, 1)
                if slot == WEIGH_SLOT and "t" in rows:
                    keep_weighed(rows["t"], AG - 1)
                if slot > 16 and slot % 16 == WEIGH_SLOT and "a" in rows:
                    keep_weighed(rows["a"], slot // 16 - 1)

            pieces = {"xnT": copy_out(xnT_hi[:, :], ps0[:, 0, :], xnT_ps, xnT_kept),
                      "shT": copy_out(shT[:, :], ps_c[:, :], shT_ps, shT_done),
                      "uT": copy_out(uT[:, :], ps_c[:, :], uT_ps, uT_done),
                      "xmT": copy_out(xmT_hi[:, :], ps_c[:, :], xmT_ps, xmT_kept),
                      "attT": copy_out(attT[:, :], ps_c[:, :], attT_ps, attT_done),
                      "gelu": gelu, "res_3": res_, "query": high(0, q_hi, "q"), "key": high(1, k_hi, "k")}
            for k in range(2 * NH):
                pieces[f"rec{k}"] = rec(k)
            for k in range(4):
                pieces[f"relu{k}"] = relu_(k)
                pieces[f"ffn1_{k}"] = ffn1(k)
                pieces[f"scale{k}"] = scale(k)
            for j in range(GC):
                pieces[f"gate{j}"] = gate(j)
            for g in range(AG):
                pieces[f"max{g}"] = split_max(g)
            pipeline(act, attention, pieces)

        @block.vector
        def _(dve):
            made = [0]

            def chain(ins):
                made[0] += 1
                ins.then_inc(su.sem, 1)
                dve.wait_ge(su.sem, made[0])

            dve.wait_ge(ws_loaded.sem, 16)
            cols = slice(0, WS_LOADED)
            chain(dve.tensor_copy(ws_hi[:, cols], ws_tmp[:, cols]))
            dve.tensor_tensor(ws_lo[:, cols], ws_tmp[:, cols], ws_hi[:, cols].bitcast(F32), ALU.subtract)\
                .then_inc(ws_ready.sem, 1)
            dve.memset(hv[:, :, :], 0.0).then_inc(ws_ready.sem, 1)
            hw8 = r_tmp[:, 0:NH]
            hw_all = hw8.unsqueeze(2).to_broadcast([P, NH, P])
            hng = r_tmp[:, NH:NH + NH * P].rearrange("p (h k) -> p h k", h=NH)
            hnb = r_tmp[:, NH + NH * P:NH + 2 * NH * P].rearrange("p (h k) -> p h k", h=NH)

            def prepare(h):
                if h == 0:
                    chain(dve.memset(cb_mask[BIAS_AT, :], -1.0))
                    chain(dve.memset(cb_mask[BIAS_AT.start:BIAS_AT.start + 1, :], 0.0))
                    chain(dve.memset(ones2.bitcast(F32), 1.0))
                    dve.wait_ge(cb_loaded.sem, 16)
                    chain(dve.tensor_copy(cb_hi.bitcast(F32R), cb_raw))
                elif h == 1:
                    chain(dve.scalar_tensor_tensor(out=cb_split, in0=cb_hi, scalar=cb_mask[BIAS_AT, 0:1], in1=cb_raw,
                                                   op0=ALU.mult, op1=ALU.add))
                elif h == 2:
                    dve.wait_ge(r_loaded.sem, 32)
                    chain(dve.tensor_tensor(pb2[:, :], rowv[:, R_COLS["proj"]:R_COLS["proj"] + P],
                                            rowv[:, R_COLS["r2"]:R_COLS["r2"] + P], ALU.add))
                    chain(dve.tensor_scalar(hw8, hw8, 1.0 / NH, None, ALU.mult))
                elif h == 3:
                    chain(dve.tensor_tensor(hw_g[:, :].rearrange("p (h k) -> p h k", h=NH), hng, hw_all, ALU.mult))
                elif h == 4:
                    chain(dve.tensor_tensor(hnb, hnb, hw_all, ALU.mult))
                elif h == 5:
                    chain(dve.tensor_reduce(hw_b[:, :], hnb.rearrange("p h k -> p k h"), AX.X, ALU.add))
                    dve.memset(cb_mask[BIAS_AT, :], 0.0).then_inc(heads_ready.sem, 1)
                elif h == 6:
                    dve.wait_ge(wi_loaded.sem, 16)
                    chain(dve.tensor_scalar(whole, wi[:, 0:2 * GC * P], DEQUANT, None, ALU.mult))
                    chain(dve.tensor_copy(ws_hi[:, WS_LOADED:WS_TOTAL], whole))
                elif h == 7:
                    chain(dve.tensor_tensor(ws_lo[:, WS_LOADED:WS_TOTAL], whole,
                                            ws_hi[:, WS_LOADED:WS_TOTAL].bitcast(F32), ALU.subtract))
                    dve.tensor_scalar(w_down[:, :], wi[:, 2 * GC * P:3 * GC * P], DEQUANT, None, ALU.mult)\
                        .then_inc(const_ready.sem, 1)

            def first_stats(src, ready, ready_n, buf, stats):
                def piece(r, rows):
                    dve.wait_ge(ready.sem, ready.of(r, ready_n))
                    for t in range(TT // 2):
                        dve.bn_stats(buf[:, t, 0:6], src[:, t, :]).then_inc(stats.sem, 1)
                return piece

            def norm_stats(src, buf, stats, var, veps):
                def piece(r, rows):
                    for t in range(TT // 2, TT):
                        dve.bn_stats(buf[:, t, 0:6], src[:, t, :]).then_inc(stats.sem, 1)
                    dve.wait_ge(stats.sem, stats.of(r, TT))
                    dve.memset(buf[:, :, 8], EPS)
                    for t in range(TT):
                        dve.bn_aggr(buf[:, t, 6:8], buf[:, t, 0:6]).then_inc(var.sem, 1)
                    dve.wait_ge(var.sem, var.of(r, TT))
                    dve.tensor_tensor(buf[:, :, 8], buf[:, :, 7], buf[:, :, 8], ALU.add).then_inc(veps.sem, 1)
                    dve.tensor_scalar(buf[:, :, 10], buf[:, :, 6], -1.0, None, ALU.mult).then_inc(veps.sem, 1)
                return piece

            def rest(hi, lo, ps, kept, done):
                def piece(r, rows):
                    dve.wait_ge(kept.sem, kept.of(r, 1))
                    dve.tensor_tensor(lo[:, :], ps, hi[:, :].bitcast(F32), ALU.subtract).then_inc(done.sem, 1)
                return piece

            def scan(h):
                def piece(r, rows):
                    dve.wait_ge(decay_done.sem, decay_done.of(r, h + 1))
                    dve.wait_ge(drive_done.sem, drive_done.of(r, h + 1))
                    dve.tensor_tensor_scan(hs[:, h, :], decay[:, h % 2, :], drive[:, h % 2, :], 0.0,
                                           ALU.mult, ALU.add).then_inc(scan_done.sem, 1)
                    if isinstance(r, int) and r == 0:
                        prepare(h)
                return piece

            def dx_(r, rows):
                dve.wait_ge(dx_ps.sem, dx_ps.of(r, 1))
                dve.tensor_tensor(dx[:, :, :], ps0[:, 1, :].rearrange("p (t k) -> p t k", t=TT), along("d"),
                                  ALU.add).then_inc(dx_done.sem, 1)

            def moments(k):
                def piece(r, rows):
                    dve.wait_ge(prod_done.sem, prod_done.of(r, k + 1))
                    for h in range(4):
                        ins = dve.bn_stats(hst[:, 4 * k + h, :], prod[:, k // 2, 4 * (k % 2) + h, :])
                    ins.then_inc(head_stats.sem, 1)
                return piece

            def head(k):
                t, half = divmod(k, 2)

                def piece(r, rows):
                    if k == 0:
                        dve.wait_ge(dx_done.sem, dx_done.of(r, 1))
                    dve.wait_ge(head_ps.sem, head_ps.of(r, k + 1))
                    dve.tensor_tensor(prod[:, t, 4 * half:4 * half + 4, :],
                                      ps0[:, half, :].rearrange("p (h k) -> p h k", h=4),
                                      dx[:, t, :].unsqueeze(1).to_broadcast([P, 4, P]), ALU.mult)\
                        .then_inc(prod_done.sem, 1)
                return piece

            def norm(t):
                c = slice(t * NH, (t + 1) * NH)

                def piece(r, rows):
                    dve.wait_ge(head_stats.sem, head_stats.of(r, 2 * t + 2))
                    dve.tensor_tensor(hv[:, 0, c], hst[:, c, 1], hst[:, c, 4], ALU.add).then_inc(head_var.sem, 1)
                    dve.tensor_tensor(hv[:, 1, c], hst[:, c, 1], hst[:, c, 4], ALU.subtract).then_inc(head_var.sem, 1)
                    dve.tensor_tensor(hv[:, 2, c], hst[:, c, 2], hst[:, c, 5], ALU.add).then_inc(head_var.sem, 1)
                    dve.wait_ge(head_var.sem, head_var.of(r, 7 * t + 3))
                    dve.tensor_scalar(hv[:, 7, c], hv[:, 0, c], -0.5, None, ALU.mult).then_inc(head_var.sem, 1)
                    dve.tensor_scalar(hv[:, 3, c], hv[:, 2, c], 1.0 / P, EPS, ALU.mult, ALU.add)\
                        .then_inc(head_var.sem, 1)
                    dve.scalar_tensor_tensor(out=hv[:, 4, c], in0=hv[:, 1, c], scalar=0.25, in1=hv[:, 1, c],
                                             op0=ALU.mult, op1=ALU.mult).then_inc(head_var.sem, 1)
                    dve.wait_ge(head_var.sem, head_var.of(r, 7 * t + 6))
                    dve.tensor_tensor(hv[:, 5, c], hv[:, 3, c], hv[:, 4, c], ALU.add).then_inc(head_var.sem, 1)
                return piece

            def sum_(k):
                t, part = k // 2, slice(k % 2 * P // 2, (k % 2 + 1) * P // 2)

                def piece(r, rows):
                    dve.wait_ge(head_added.sem, head_added.of(r, t + 1))
                    dve.tensor_reduce(hsum[:, t, part], prod[:, t, :, part].rearrange("p h k -> p k h"), AX.X, ALU.add)\
                        .then_inc(sum_done.sem, 1)
                return piece

            def z_(r, rows):
                dve.wait_ge(z_ps.sem, z_ps.of(r, 1))
                dve.tensor_tensor(z[:, :, :], ps_c[:, :].rearrange("p (t k) -> p t k", t=TT), along("wout"),
                                  ALU.add).then_inc(z_done.sem, 1)

            def u_(r, rows):
                dve.wait_ge(zn_done.sem, zn_done.of(r, 1))
                dve.tensor_tensor(zn[:, :, :], zn[:, :, :], along("ng"), ALU.mult).then_inc(zg_done.sem, 1)

            def u2(r, rows):
                dve.wait_ge(zg_done.sem, zg_done.of(r, 1))
                dve.wait_ge(z_b_done.sem, z_b_done.of(r, 1))
                dve.tensor_tensor(zn[:, :, :], zn[:, :, :], z_b[:, :, :], ALU.add).then_inc(u_done.sem, 1)

            def ffn2(r, rows):
                dve.wait_ge(f2_ps.sem, f2_ps.of(r, 1))
                dve.wait_ge(uT_done.sem, uT_done.of(r, 1))
                dve.scalar_tensor_tensor(out=hT[:, :], in0=ps_c[:, :], scalar=bcol("f2"), in1=uT[:, :],
                                         op0=ALU.add, op1=ALU.add).then_inc(hT_done.sem, 1)

            def x1_(r, rows):
                dve.wait_ge(x1_ps.sem, x1_ps.of(r, TT))
                dve.wait_ge(x_bias_done.sem, x_bias_done.of(r, 1))
                dve.tensor_tensor(flat(x1), ps_c[:, :], flat(x_bias), ALU.add).then_inc(x1_done.sem, 1)

            def low(part, hi, lo, name):
                def piece(r, rows):
                    dve.wait_ge(qk_hi.sem, qk_hi.of(r, part + 1))
                    dve.scalar_tensor_tensor(out=lo[:, :], in0=ps_c[:, :], scalar=bcol(name),
                                             in1=hi[:, :].bitcast(F32), op0=ALU.add, op1=ALU.subtract)\
                        .then_inc(qk_lo.sem, 1)
                return piece

            def split_max(g):
                def piece(r, rows):
                    dve.wait_ge(s_max.sem, s_max.of(r, 16 * (g + 1)))
                    dve.tensor_copy(mx_split[:, :, 0, :], mx[:, g, :, :]).then_inc(mx_high.sem, 1)
                    dve.wait_ge(mx_high.sem, mx_high.of(r, g + 1))
                    dve.tensor_tensor(mx_split[:, :, 1, :], mx[:, g, :, :], mx_split[:, :, 0, :].bitcast(F32),
                                      ALU.subtract).then_inc(mx_low.sem, 1)
                return piece

            def values(r, rows):
                dve.wait_ge(v_ps.sem, v_ps.of(r, 1))
                b = rowv[:, R_COLS["v"]:R_COLS["v"] + P].rearrange("p (h d) -> p h d", d=HD).unsqueeze(1)
                dve.tensor_tensor(vv[:, :, :, 0:HD], ps_c[:, :].rearrange("p (t h d) -> p t h d", t=TT, d=HD),
                                  b.to_broadcast([P, TT, 4 * AG, HD]), ALU.add).then_inc(v_done.sem, 1)

            def att_(g):
                def piece(r, rows):
                    dve.wait_ge(o_ps.sem, o_ps.of(r, g + 1))
                    o = ps_st[:, 1, :].rearrange("p (t h r) -> p t h r", t=TT, h=4)
                    dve.reciprocal(rden[:, :, :], o[:, :, :, HD]).then_inc(rden_done.sem, 1)
                    dve.wait_ge(rden_done.sem, rden_done.of(r, g + 1))
                    dve.tensor_tensor(att[:, :, 32 * g:32 * g + 32].rearrange("p t (h d) -> p t h d", h=4),
                                      o[:, :, :, 0:HD], rden[:, :, :].unsqueeze(3).to_broadcast([P, TT, 4, HD]),
                                      ALU.mult).then_inc(att_done.sem, 1)
                return piece

            def gate(j):
                def piece(r, rows):
                    dve.wait_ge(tanh_done.sem, tanh_done.of(r, j + 1))
                    dve.scalar_tensor_tensor(out=g_tanh[:, :], in0=g_tanh[:, :], scalar=1.0, in1=ps_c[:, :],
                                             op0=ALU.add, op1=ALU.mult).then_inc(g_lin_done.sem, 1)
                return piece

            def up(j):
                def piece(r, rows):
                    dve.wait_ge(up_ps.sem, up_ps.of(r, j + 1))
                    dve.scalar_tensor_tensor(out=ffh[:, j, :], in0=g_tanh[:, :], scalar=0.5, in1=ps_c[:, :],
                                             op0=ALU.mult, op1=ALU.mult).then_inc(ffh_done.sem, 1)
                return piece

            def store(r, rows):
                dve.wait_ge(y_ps.sem, y_ps.of(r, 1))
                dve.wait_ge(res_held_done.sem, res_held_done.of(r, 1))
                dve.tensor_tensor(flat(y), ps_c[:, :], flat(res_held), ALU.add).then_inc(y_done.sem, 1)

            def attention(slot, rows):
                n = (slot + S_AHEAD) % SLOTS
                who = "a" if slot + S_AHEAD < SLOTS else "c"
                if who in rows:
                    g, qt, h = n // 16, n // 4 % TT, n % 4
                    dve.wait_ge(s_ps.sem, s_ps.of(rows[who], n + 1))
                    dve.tensor_reduce(mx[:, g, qt, h:h + 1], ps_s[:, n % 2, :], AX.X, ALU.max).then_inc(s_max.sem, 1)
                    if n % 16 == 15:
                        split_max(g)(rows[who], rows)
                if slot == ATT_SLOT and "t" in rows:
                    att_(AG - 1)(rows["t"], rows)
                elif slot > 16 and slot % 16 == ATT_SLOT and "a" in rows:
                    att_(slot // 16 - 1)(rows["a"], rows)

            pieces = {"ln1a": first_stats(xin, x_loaded, 16, ln1, ln1_stats),
                      "ln1": norm_stats(xin, ln1, ln1_stats, ln1_var, ln1_veps),
                      "xnT": rest(xnT_hi, xnT_lo, ps0[:, 0, :], xnT_kept, xnT_done),
                      "xmT": rest(xmT_hi, xmT_lo, ps_c[:, :], xmT_kept, xmT_done),
                      "dx": dx_, "z": z_,
                      "lnza": first_stats(z, z_done, 1, lnz, lnz_stats),
                      "lnz": norm_stats(z, lnz, lnz_stats, lnz_var, lnz_veps), "u": u_, "u2": u2,
                      "ffn2_3": ffn2, "x1_3": x1_,
                      "ln2a": first_stats(x1, x1_done, 1, ln2, ln2_stats),
                      "ln2": norm_stats(x1, ln2, ln2_stats, ln2_var, ln2_veps),
                      "query": low(0, q_hi, q_lo, "q"), "key": low(1, k_hi, k_lo, "k"), "values": values, "store": store}
            for h in range(NH):
                pieces[f"rec{2 * h + 1}"] = scan(h)
                pieces[f"head{h}"] = head(h)
                pieces[f"moments{h}"] = moments(h)
                pieces[f"sum{h}"] = sum_(h)
            for t in range(TT):
                pieces[f"norm{t}"] = norm(t)
            for j in range(GC):
                pieces[f"gate{j}"] = gate(j)
                pieces[f"up{j}"] = up(j)
            late = ["values", "store", "dx", "query", "key"] + [f"{name}{k}" for name, count in (("rec", 2 * NH), ("head", NH))
                                              for k in range(count)]
            pipeline(dve, attention, pieces, late)

        @block.gpsimd
        def _(pool):
            pool.memset(ident[:, :], 0.0).then_inc(pool_const.sem, 1)
            pool.memset(k_st[:, :, :].bitcast(F32), 0.0).then_inc(pool_const.sem, 1)
            pool.memset(q_st[:, :, :].bitcast(F32), 0.0).then_inc(pool_const.sem, 1)
            pool.memset(neg_half[:, :], -0.5).then_inc(pool_const.sem, 1)
            pool.memset(per_head[:, :], 1.0 / NH).then_inc(pool_const.sem, 1)
            pool.memset(vv[:, :, :, :], 0.0).then_inc(pool_const.sem, 1)
            pool.wait_ge(pool_const.sem, POOL_CONST - 4)
            pool.memset(zeros, 0.0).then_inc(pool_const.sem, 1)
            pool.wait_ge(pool_const.sem, POOL_CONST - 3)
            pool.memset(ones_row, 1.0).then_inc(pool_const.sem, 1)
            pool.wait_ge(pool_const.sem, POOL_CONST - 2)
            pool.affine_select(out=ident[:, :], in_=ident[:, :], compare_op=ALU.not_equal, fill=1.0, base=0,
                               pattern=[[-1, P]], channel_multiplier=1).then_inc(pool_const.sem, 1)
            pool.memset(vv[:, :, :, HD:HD + 1], 1.0).then_inc(pool_const.sem, 1)
            pool.wait_ge(pool_const.sem, POOL_CONST)
            pool.wait_ge(r_loaded.sem, 32)

            def normalise(dst, src, buf, veps, rstd, done):
                def piece(r, rows):
                    if done is xn_done and has_past(r):
                        pool.wait_ge(xnT_ps.sem, xnT_ps.of(r - 1, 1))
                    elif done is zn_done and has_past(r):
                        pool.wait_ge(xmT_ps.sem, xmT_ps.of(r - 1, 1))
                    elif done is xm_done:
                        pool.wait_ge(uT_ps.sem, uT_ps.of(r, 1))
                    pool.wait_ge(veps.sem, veps.of(r, 2))
                    pool.tensor_tensor(buf[:, :, 9], buf[:, :, 8], neg_half[:, 0:TT], ALU.pow).then_inc(rstd.sem, 1)
                    pool.wait_ge(rstd.sem, rstd.of(r, 1))
                    pool.tensor_tensor(buf[:, :, 11], buf[:, :, 10], buf[:, :, 9], ALU.mult).then_inc(rstd.sem, 1)
                    pool.wait_ge(pool_const.sem, 1)
                    pool.wait_ge(rstd.sem, rstd.of(r, 2))
                    for t in range(TT):
                        ins = pool.tensor_scalar(dst[:, t, :], src[:, t, :], buf[:, t, 9:10], buf[:, t, 11:12],
                                                 ALU.mult, ALU.add)
                    ins.then_inc(done.sem, 1)
                return piece

            def x_bias_(r, rows):
                if isinstance(r, int) and r == 0:
                    pool.wait_ge(heads_ready.sem, 1)
                if has_past(r):
                    pool.wait_ge(x1_done.sem, x1_done.of(r - 1, 1))
                pool.tensor_tensor(x_bias[:, :, :], xin[:, :, :], pb2[:, :].unsqueeze(1).to_broadcast([P, TT, P]),
                                   ALU.add).then_inc(x_bias_done.sem, 1)

            def dx_(r, rows):
                if isinstance(r, int) and r == 0:
                    pool.wait_ge(heads_ready.sem, 1)
                pool.wait_ge(dx_done.sem, dx_done.of(r, 1))
                pool.tensor_tensor(flat(dx_b), flat(dx), per_head[:, :].to_broadcast([P, TT * P]), ALU.mult)\
                    .then_inc(dx_b_done.sem, 1)
                pool.wait_ge(dx_b_done.sem, dx_b_done.of(r, 1))
                pool.tensor_tensor(dx_b[:, :, :], dx_b[:, :, :], hw_b[:, :].unsqueeze(1).to_broadcast([P, TT, P]),
                                   ALU.add).then_inc(dx_b_done.sem, 1)

            def norm(t):
                c = slice(t * NH, (t + 1) * NH)

                def piece(r, rows):
                    pool.wait_ge(head_var.sem, head_var.of(r, 7 * t + 7))
                    pool.tensor_tensor(hv[:, 6, c], hv[:, 5, c], neg_half[:, c], ALU.pow).then_inc(head_rstd.sem, 1)
                    pool.wait_ge(head_rstd.sem, head_rstd.of(r, t + 1))
                    pool.tensor_tensor(hv[:, 0, c], hv[:, 7, c], hv[:, 6, c], ALU.mult).then_inc(head_shift.sem, 1)
                    pool.wait_ge(pool_const.sem, 1)
                    pool.wait_ge(head_shift.sem, head_shift.of(r, t + 1))
                    for h in range(NH // 2):
                        k = t * NH + h
                        ins = pool.tensor_scalar(prod[:, t, h, :], prod[:, t, h, :], hv[:, 6, k:k + 1],
                                                 hv[:, 0, k:k + 1], ALU.mult, ALU.add)
                    ins.then_inc(head_norm.sem, 1)
                    pool.wait_ge(head_norm.sem, head_norm.of(r, t + 1))
                    pool.wait_ge(head_norm_act.sem, head_norm_act.of(r, t + 1))
                    pool.tensor_tensor(prod[:, t, :, :].rearrange("p h k -> p (h k)"),
                                       prod[:, t, :, :].rearrange("p h k -> p (h k)"), hw_g[:, :],
                                       ALU.mult).then_inc(head_scaled.sem, 1)
                    pool.wait_ge(head_scaled.sem, head_scaled.of(r, t + 1))
                    pool.tensor_tensor(prod[:, t, 0, :], prod[:, t, 0, :], dx_b[:, t, :], ALU.add)\
                        .then_inc(head_added.sem, 1)
                return piece

            def z_(r, rows):
                pool.wait_ge(z_done.sem, z_done.of(r, 1))
                pool.tensor_tensor(z_b[:, :, :], z[:, :, :], along("nb"), ALU.add).then_inc(z_b_done.sem, 1)

            def x1_(r, rows):
                if has_past(r):
                    pool.wait_ge(res_held_done.sem, res_held_done.of(r - 1, 1))
                pool.wait_ge(x1_done.sem, x1_done.of(r, 1))
                pool.tensor_tensor(x1_b[:, :, :], x1[:, :, :], along("ap"), ALU.add).then_inc(x1_b_done.sem, 1)

            def hold(r, rows):
                pool.wait_ge(res_done.sem, res_done.of(r, 1))
                if has_past(r):
                    pool.wait_ge(stored.sem, stored.of(r - 1, 16))
                pool.tensor_tensor(flat(res_held), flat(res), flat(x1_b), ALU.add).then_inc(res_held_done.sem, 1)

            pieces = {"ln1": normalise(xn, xin, ln1, ln1_veps, ln1_rstd, xn_done),
                      "lnz": normalise(zn, z, lnz, lnz_veps, lnz_rstd, zn_done),
                      "ln2": normalise(xm, x1, ln2, ln2_veps, ln2_rstd, xm_done),
                      "x_bias": x_bias_, "dx": dx_, "z": z_,
                      "x1_3": x1_, "hold": hold}
            for t in range(TT):
                pieces[f"norm{t}"] = norm(t)
            pipeline(pool, lambda slot, rows: None, pieces)


def kernel(**inputs):
    import concourse.bacc as bacc
    from concourse.bass_utils import run_bass_kernel_spmd

    a = {k: np.asarray(v) for k, v in inputs.items()}

    def g0(name):
        return a["L0_attn_" + name]

    def heads(m):
        return m.transpose(2, 0, 1).reshape(P, NH * P)

    def chunks(m):
        return m.reshape(-1, P, m.shape[1]).transpose(1, 0, 2).reshape(P, -1)

    parts = {"wa": heads(g0("Wa_w")), "wb": heads(g0("Wb_w")), "c": heads(g0("C_w")), "d": g0("D_w").T,
             "wout": g0("Wout_w").T, "f1": g0("ffn1_w").T, "f2": chunks(g0("ffn2_w").T), "proj": g0("proj_w").T,
             "r1": a["L0_ffn_W1"], "r2": chunks(a["L0_ffn_W2"]), "qkv": a["L1_attn_w_qkv"], "ap": a["L1_attn_w_proj"]}
    w_pack = np.ascontiguousarray(np.concatenate([parts[n] for n in W_COLS], axis=1))
    ws_pack = np.ascontiguousarray(np.concatenate([parts[n] for n in WS_COLS if n in parts], axis=1))
    wi_pack = np.ascontiguousarray(np.concatenate(
        [a["L1_ffn_w_gate"].T, a["L1_ffn_w_up"].T, chunks(a["L1_ffn_w_down"].T)], axis=1))
    bqkv = a["L1_attn_b_qkv"]
    cols = {"wa": g0("Wa_b").T, "wb": g0("Wb_b").T, "f1": g0("ffn1_b").reshape(FC, P).T, "f2": g0("ffn2_b")[:, None],
            "r1": a["L0_ffn_b1"].reshape(FC, P).T, "q": bqkv[0:P, None], "k": bqkv[P:2 * P, None]}
    b_pack = np.ascontiguousarray(np.concatenate([cols[n] for n in B_COLS], axis=1))
    rows = {"d": g0("D_b"), "wout": g0("Wout_b"), "ng": g0("norm_g"), "nb": g0("norm_b"), "proj": g0("proj_b"),
            "r2": a["L0_ffn_b2"], "v": bqkv[2 * P:], "ap": a["L1_attn_b_proj"], "hw": g0("head_w"),
            "hng": g0("hn_g").reshape(-1), "hnb": g0("hn_b").reshape(-1)}
    r_pack = np.ascontiguousarray(np.concatenate([rows[n] for n in R_COLS])[None, :])
    arrays = {"x": np.ascontiguousarray(g0("emb").reshape(ROWS * L, P)), "w_pack": w_pack, "ws_pack": ws_pack,
              "wi_pack": wi_pack,
              "b_pack": b_pack, "r_pack": r_pack, "cb": np.ascontiguousarray(g0("C_b").reshape(1, NH * P))}

    nc = bacc.Bacc("TRN2", target_bir_lowering=False, num_devices=1)
    args = [nc.dram_tensor("in_" + n, v.shape, mybir.dt.from_np(v.dtype), kind="ExternalInput").ap()
            for n, v in arrays.items()]
    args.append(nc.dram_tensor("out", (ROWS * L, P), F32, kind="ExternalOutput").ap())
    two_block_model(nc, *args)
    r = run_bass_kernel_spmd(nc, [{"in_" + n: v for n, v in arrays.items()}], core_ids=[0])
    return r.results[0]["out"].reshape(ROWS, L, P)
```
